# Optimizing a Trainium2 kernel written in Bass

```python
import numpy as np
import jax
import jax.numpy as jnp

def _softmax(x, axis=-1):
    return jax.nn.softmax(x, axis=axis)

def _gelu(x):
    return jax.nn.gelu(x, approximate=True)

def _silu(x):
    return jax.nn.silu(x)

def _sigmoid(x):
    return jax.nn.sigmoid(x)

def _layernorm(x, axis=-1, eps=1e-05):
    m = jnp.mean(x, axis=axis, keepdims=True)
    v = jnp.var(x, axis=axis, keepdims=True)
    return (x - m) / jnp.sqrt(v + eps)

def _scatter_add(tgt, idx, src, axis=0):
    return tgt.at[idx].add(src)

def _segment_sum(src, seg, n):
    return jax.ops.segment_sum(src, seg, n)
kernel_name = 'mk_seq_postln_d1_jaxref_r4_eba57a'

def setup_inputs(seed: int=0):
    np.random.seed(seed)
    _w = jnp.asarray

    def _L0_attn_setup():
        import jax, jax.numpy as jnp
        import numpy as np
        B, S, H = (2, 512, 512)
        NH, HD = (16, H // 16)
        WINDOW = 256
        THETA = 10000.0
        EPS = 1e-06

        def rmsnorm(x, w):
            var = jnp.mean(jnp.square(x), axis=-1, keepdims=True)
            return x * jax.lax.rsqrt(var + EPS) * w

        def rope(x, cos, sin):
            d2 = x.shape[-1] // 2
            x1, x2 = (x[..., :d2], x[..., d2:])
            c = cos[None, :, None, :]
            s = sin[None, :, None, :]
            return jnp.concatenate([x1 * c - x2 * s, x2 * c + x1 * s], axis=-1)
        key = jax.random.key(seed)
        k1, k2, k3 = jax.random.split(key, 3)
        sc = 1.0 / np.sqrt(H)
        return {'hidden_states': jax.random.normal(k1, (B, S, H), dtype=jnp.float32), 'Wqkv': jax.random.normal(k2, (H, 3 * H), dtype=jnp.float32) * sc, 'q_norm_w': jnp.ones((H,), dtype=jnp.float32), 'k_norm_w': jnp.ones((H,), dtype=jnp.float32), 'Wo': jax.random.normal(k3, (H, H), dtype=jnp.float32) * sc}
    _L0_attn_in = _L0_attn_setup()

    def _L0_ffn_setup():
        import jax, jax.numpy as jnp
        import numpy as np
        H = 512
        I_MOE = 352
        I_SH = 1408
        E = 8
        TOP_K = 2
        B, S = (1, 512)

        def _silu_and_mul(gu, inter):
            return jax.nn.silu(gu[..., :inter]) * gu[..., inter:]
        key = jax.random.key(seed)
        ks = jax.random.split(key, 7)
        sc = 0.02
        return {'hidden_states': jax.random.normal(ks[0], (B, S, H), jnp.float32), 'W_router': jax.random.normal(ks[1], (E, H), jnp.float32) * sc, 'W_sgate': jax.random.normal(ks[2], (1, H), jnp.float32) * sc, 'Ws_gate_up': jax.random.normal(ks[3], (H, 2 * I_SH), jnp.float32) * sc, 'Ws_down': jax.random.normal(ks[4], (I_SH, H), jnp.float32) * sc, 'We_gate_up': jax.random.normal(ks[5], (E, H, 2 * I_MOE), jnp.float32) * sc, 'We_down': jax.random.normal(ks[6], (E, I_MOE, H), jnp.float32) * sc}
    _L0_ffn_in = _L0_ffn_setup()
    _d = {'L0_attn_hidden_states': _L0_attn_in['hidden_states'], 'L0_attn_Wqkv': _L0_attn_in['Wqkv'], 'L0_attn_q_norm_w': _L0_attn_in['q_norm_w'], 'L0_attn_k_norm_w': _L0_attn_in['k_norm_w'], 'L0_attn_Wo': _L0_attn_in['Wo'], 'L0_ffn_W_router': _L0_ffn_in['W_router'], 'L0_ffn_W_sgate': _L0_ffn_in['W_sgate'], 'L0_ffn_Ws_gate_up': _L0_ffn_in['Ws_gate_up'], 'L0_ffn_Ws_down': _L0_ffn_in['Ws_down'], 'L0_ffn_We_gate_up': _L0_ffn_in['We_gate_up'], 'L0_ffn_We_down': _L0_ffn_in['We_down']}
    _x0 = _d['L0_attn_hidden_states']
    _d['L0_attn_hidden_states'] = jax.random.normal(jax.random.fold_in(jax.random.key(seed), 1), (1, 2048, 512), dtype=_x0.dtype)
    del _x0
    return _d

def reference(L0_attn_hidden_states, L0_attn_Wqkv, L0_attn_q_norm_w, L0_attn_k_norm_w, L0_attn_Wo, L0_ffn_W_router, L0_ffn_W_sgate, L0_ffn_Ws_gate_up, L0_ffn_Ws_down, L0_ffn_We_gate_up, L0_ffn_We_down):

    def _L0_attn_ref(hidden_states, Wqkv, q_norm_w, k_norm_w, Wo):
        import jax, jax.numpy as jnp
        import numpy as np
        B, S, H = (2, 512, 512)
        NH, HD = (16, H // 16)
        WINDOW = 256
        THETA = 10000.0
        EPS = 1e-06

        def rmsnorm(x, w):
            var = jnp.mean(jnp.square(x), axis=-1, keepdims=True)
            return x * jax.lax.rsqrt(var + EPS) * w

        def rope(x, cos, sin):
            d2 = x.shape[-1] // 2
            x1, x2 = (x[..., :d2], x[..., d2:])
            c = cos[None, :, None, :]
            s = sin[None, :, None, :]
            return jnp.concatenate([x1 * c - x2 * s, x2 * c + x1 * s], axis=-1)
        b, s, h = hidden_states.shape
        qkv = hidden_states @ Wqkv
        q, k, v = jnp.split(qkv, 3, axis=-1)
        q = rmsnorm(q, q_norm_w)
        k = rmsnorm(k, k_norm_w)
        q = q.reshape(b, s, NH, HD)
        k = k.reshape(b, s, NH, HD)
        v = v.reshape(b, s, NH, HD)
        inv_freq = 1.0 / THETA ** (jnp.arange(0, HD, 2, dtype=jnp.float32) / HD)
        freqs = jnp.arange(s, dtype=jnp.float32)[:, None] * inv_freq[None, :]
        cos, sin = (jnp.cos(freqs), jnp.sin(freqs))
        q = rope(q, cos, sin)
        k = rope(k, cos, sin)
        q_idx = jnp.arange(s)[:, None]
        k_idx = jnp.arange(s)[None, :]
        mask = (q_idx >= k_idx) & (q_idx - k_idx <= WINDOW - 1)
        scale = 1.0 / np.sqrt(HD)
        scores = jnp.einsum('bqhd,bkhd->bhqk', q, k) * scale
        scores = jnp.where(mask[None, None, :, :], scores, jnp.float32(-jnp.inf))
        probs = jax.nn.softmax(scores, axis=-1)
        o = jnp.einsum('bhqk,bkhd->bqhd', probs, v).reshape(b, s, h)
        return o @ Wo

    def _L0_ffn_ref(hidden_states, W_router, W_sgate, Ws_gate_up, Ws_down, We_gate_up, We_down):
        import jax, jax.numpy as jnp
        import numpy as np
        H = 512
        I_MOE = 352
        I_SH = 1408
        E = 8
        TOP_K = 2
        B, S = (1, 512)

        def _silu_and_mul(gu, inter):
            return jax.nn.silu(gu[..., :inter]) * gu[..., inter:]
        orig_shape = hidden_states.shape
        x = hidden_states.reshape(-1, H)
        T = x.shape[0]
        logits = x @ W_router.T
        probs = jax.nn.softmax(logits.astype(jnp.float32), axis=-1)
        rw, sel = jax.lax.top_k(probs, TOP_K)
        rw = rw.astype(x.dtype)
        combine = jnp.zeros((T, E), x.dtype).at[jnp.arange(T)[:, None], sel].add(rw)
        sh = _silu_and_mul(x @ Ws_gate_up, I_SH) @ Ws_down
        shared_out = sh * jax.nn.sigmoid(x @ W_sgate.T)
        gu = jnp.einsum('th,ehi->eti', x, We_gate_up)
        h = _silu_and_mul(gu, I_MOE)
        eo = jnp.einsum('eti,eih->eth', h, We_down)
        sparse_out = jnp.einsum('eth,te->th', eo, combine)
        return (shared_out + sparse_out).reshape(orig_shape)
    x = L0_attn_hidden_states
    x = _layernorm(x + _L0_attn_ref(x, L0_attn_Wqkv, L0_attn_q_norm_w, L0_attn_k_norm_w, L0_attn_Wo), axis=-1)
    x = _layernorm(x + _L0_ffn_ref(x, L0_ffn_W_router, L0_ffn_W_sgate, L0_ffn_Ws_gate_up, L0_ffn_Ws_down, L0_ffn_We_gate_up, L0_ffn_We_down), axis=-1)
    return x

_drawn_inputs = setup_inputs


def setup_inputs(seed=0):
    import zlib

    import numpy as np

    out = dict(_drawn_inputs(seed))
    spreads = {'L0_attn_q_norm_w': (1.0, 0.557), 'L0_attn_k_norm_w': (1.0, 0.567)}
    factors = {'L0_ffn_W_router': 5.549,
     'L0_ffn_W_sgate': 43.47,
     'L0_ffn_We_gate_up': 4.738,
     'L0_ffn_We_down': 4.735,
     'L0_ffn_Ws_gate_up': 3.908,
     'L0_ffn_Ws_down': 3.913}
    for name, (base, spread) in spreads.items():
        noise = np.random.default_rng([zlib.crc32(name.encode()), seed]).standard_normal(out[name].shape)
        drawn = base * np.exp(spread * noise) if base else spread * noise
        out[name] = jnp.asarray(drawn.astype(out[name].dtype))
    for name, factor in factors.items():
        out[name] = (out[name] * factor).astype(out[name].dtype)
    return out
```

```python
import numpy as np
import concourse.bass as bass
from concourse import mybir
from contextlib import ExitStack

FP32 = mybir.dt.float32
FP32R = mybir.dt.float32r
ALU = mybir.AluOpType
ACT = mybir.ActivationFunctionType

P = 128
S = 2048
H = 512
NH, HD = 16, 32
KT = H // P
NB = S // P
WINDOW = 256
WB = WINDOW // P + 1
RING = 4
GROUPS = NH // 4
SCALE = 1.0 / HD ** 0.5
RMS_EPS, LN_EPS = 1e-6, 1e-5
NEG = -1e30
THETA = 10000.0

E, TOP_K, I_MOE, I_SH = 8, 2, 352, 1408
NR = E + 1


def wait(engine, semaphore, value):
    if isinstance(value, int) and value <= 0:
        return
    engine.wait_ge(semaphore, value)


def wait_apart(engine, semaphore, value, passed):
    wait(engine, semaphore, value)
    if not isinstance(value, int):
        engine.sem_inc(passed, 1)


def window_runs(j):
    slots = [(j - WB + 1 + w) % RING for w in range(WB)]
    runs = []
    for w, slot in enumerate(slots):
        if runs and runs[-1][1] + runs[-1][2] == slot:
            runs[-1][2] += 1
        else:
            runs.append([w, slot, 1])
    return runs, slots


def attention_phase(nc, x, Wqkv, q_w, k_w, Wo, trig, ident_in, masks_in, sel_in, x1_dram, x1T):
    with ExitStack() as ctx:
        def sb(name, shape, dt=FP32):
            return ctx.enter_context(nc.sbuf_tensor(name, shape, dt))

        def sem(name):
            return ctx.enter_context(nc.semaphore(name))

        ident = sb("ident", [P, P])
        masks = sb("masks", [P, 3, WB * P])
        sel = sb("sel", [NH, KT, P])
        qw_b, kw_b = sb("qw_b", [P, H]), sb("kw_b", [P, H])
        wqkv_hi, wqkv_lo = sb("wqkv_hi", [P, KT, 3 * H], FP32R), sb("wqkv_lo", [P, KT, 3 * H], FP32R)
        wo_hi, wo_lo = sb("wo_hi", [P, KT, H], FP32R), sb("wo_lo", [P, KT, H], FP32R)
        half = sb("half", [P, 1])
        x_in = sb("x_in", [P, RING, H])
        cs = sb("cs", [P, RING, 2, HD])
        xT_hi, xT_lo = sb("xT_hi", [P, KT, P], FP32R), sb("xT_lo", [P, KT, P], FP32R)
        qk = sb("qk", [P, 2, H])
        rot_a, rot_b = sb("rot_a", [P, H]), sb("rot_b", [P, H])
        junk = sb("junk", [P, 1, H])
        ssq, rms = sb("ssq", [P, 2]), sb("rms", [P, 4])
        qT_hi, qT_lo = sb("qT_hi", [P, 2, KT, P], FP32R), sb("qT_lo", [P, 2, KT, P], FP32R)
        kT_hi, kT_lo = sb("kT_hi", [P, KT, RING, P], FP32R), sb("kT_lo", [P, KT, RING, P], FP32R)
        v_ring = sb("v_ring", [P, RING, H])
        prob = sb("prob", [P, 2, 4, WB * P])
        probT = sb("probT", [P, 2, 4, WB * P])
        nbias, rsum = sb("nbias", [P, 2, NH]), sb("rsum", [P, 2, NH])
        rinv, rinvT = sb("rinv", [P, NH]), sb("rinvT", [NH, P])
        r_rep = sb("r_rep", [P, H])
        oT = sb("oT", [P, H])
        oT_hi, oT_lo = sb("oT_hi", [P, KT, P], FP32R), sb("oT_lo", [P, KT, P], FP32R)
        res = sb("res", [P, H])
        bn6, mv, rstd = sb("bn6", [P, 6]), sb("mv", [P, 2]), sb("rstd", [P, 2])
        x1 = sb("x1", [P, 2, H])

        def bank(name, n=1):
            return ctx.enter_context(nc.psum_tensor(name, [P, n, H], FP32))

        score_ps = [bank(f"score_ps{i}") for i in range(2)]
        probT_ps = bank("probT_ps", 2)
        oT_ps = bank("oT_ps")
        ps_q, ps_k, ps_v = bank("ps_q"), bank("ps_k"), bank("ps_v")

        w_loaded = [sem(f"w_loaded{k}") for k in range(KT + 1)]
        const_loaded = sem("const_loaded")
        x_loaded = [sem(f"x_loaded{i}") for i in range(RING)]
        x1_stored = sem("x1_stored")
        passed = {e: sem(f"{e}_waits_passed") for e in ("dve", "pool", "sp")}
        w_hi_made, w_lo_made, cleared = sem("w_hi_made"), sem("w_lo_made"), sem("cleared")
        xT_mm, q_mm, k_mm, v_mm, qT_mm, kT_mm = map(sem, ("xT_mm", "q_mm", "k_mm", "v_mm", "qT_mm", "kT_mm"))
        score_mm, probT_mm, pv_mm = map(sem, ("score_mm", "probT_mm", "pv_mm"))
        rinvT_mm, rrep_mm, wo_mm, x1T_mm = map(sem, ("rinvT_mm", "rrep_mm", "wo_mm", "x1T_mm"))
        xT_hi_made, q_sq, k_sq, v_made, exp_made = map(sem, ("xT_hi_made", "q_sq", "k_sq", "v_made", "exp_made"))
        probT_act, rinvT_made, rrep_made, oT_hi_made = map(sem, ("probT_act", "rinvT_made", "rrep_made", "oT_hi_made"))
        x1T_made, qT_hi_made, kT_hi_made = map(sem, ("x1T_made", "qT_hi_made", "kT_hi_made"))
        xT_lo_made, q_normed, k_normed, masked = map(sem, ("xT_lo_made", "q_normed", "k_normed", "masked"))
        probT_dve, rinv_made, oT_made, oT_lo_made = map(sem, ("probT_dve", "rinv_made", "oT_made", "oT_lo_made"))
        res_made, bn_made, mv_made, x1_made = map(sem, ("res_made", "bn_made", "mv_made", "x1_made"))
        qT_lo_made, kT_lo_made = map(sem, ("qT_lo_made", "kT_lo_made"))
        q_var, k_var, q_rms, k_rms = map(sem, ("q_var", "k_var", "q_rms", "k_rms"))
        q_part, k_part, q_rot, k_rot = map(sem, ("q_part", "k_part", "q_rot", "k_rot"))
        ln_var, ln_rstd = map(sem, ("ln_var", "ln_rstd"))

        staged = x1T[:, :, :].rearrange("p k s -> p (k s)")
        wqkv_raw = staged[:, 0:KT * 3 * H].rearrange("p (k n) -> p k n", k=KT)
        wo_raw = staged[:, KT * 3 * H:].rearrange("p (k n) -> p k n", k=KT)

        def steps(engine, step):
            for s in (-1, 0, 1):
                step(s, s % RING, s // RING)
            with engine.Fori(0, 3) as i:
                for j in range(RING):
                    s0 = 2 + j
                    step(RING * i + s0, s0 % RING, i + s0 // RING)
            for s in range(14, 18):
                step(s, s % RING, s // RING)

        def has(block):
            return not isinstance(block, int) or 0 <= block < NB

        block = ctx.enter_context(nc.Block())

        @block.sync
        def _(sp):
            def load_x(n, slot):
                sp.dma_start(x_in[:, slot, :], x[bass.ts(n, P), :]).then_inc(x_loaded[slot], 16)
                sp.dma_start(cs[:, slot, :, :], trig[bass.ts(n, P), :, :]).then_inc(x_loaded[slot], 16)

            sp.dma_start(ident[:, :], ident_in).then_inc(const_loaded, 16)
            load_x(0, 0)
            for k in range(KT):
                sp.dma_start(wqkv_raw[:, k, :], Wqkv[k * P:(k + 1) * P, :]).then_inc(w_loaded[k], 16)
            sp.dma_start(qw_b[:, :], q_w.partition_broadcast(P)).then_inc(const_loaded, 16)
            sp.dma_start(kw_b[:, :], k_w.partition_broadcast(P)).then_inc(const_loaded, 16)
            sp.dma_start(masks[:, :, :], masks_in).then_inc(const_loaded, 16)
            sp.dma_start(sel[:, :, :], sel_in).then_inc(const_loaded, 16)
            sp.dma_start(wo_raw, Wo.rearrange("(k p) n -> p k n", p=P)).then_inc(w_loaded[KT], 16)
            load_x(1, 1)

            def step(s, j, turn):
                if isinstance(s, int) and s < 0:
                    return
                if has(s + 2):
                    wait(sp, res_made, s - 1)
                    wait(sp, k_rot, s - 1)
                    load_x(s + 2, (j + 2) % RING)
                if has(s - 2):
                    wait(sp, x1_made, s - 1)
                    sp.dma_start(x1_dram[bass.ts(s - 2, P), :], x1[:, j % 2, :]).then_inc(x1_stored, 16)
                    wait_apart(sp, x1_stored, 16 * (s - 1), passed["sp"])

            steps(sp, step)

        @block.gpsimd
        def _(pool):
            pool.memset(half[:, :], -0.5).then_inc(cleared, 1)
            pool.memset(v_ring[:, 2:4, :], 0.0).then_inc(cleared, 1)
            pool.memset(kT_hi[:, :, 2:4, :].bitcast(FP32), 0.0).then_inc(cleared, 1)
            pool.memset(kT_lo[:, :, 2:4, :].bitcast(FP32), 0.0).then_inc(cleared, 1)
            pool.wait_ge(cleared, 4)

            def rms_of(n, c, squares, var, rms_ready):
                wait_apart(pool, squares, n + 1, passed["pool"])
                nc.gpsimd.tensor_scalar(rms[:, 2 + c:3 + c], ssq[:, c:c + 1], 1.0 / H, RMS_EPS, ALU.mult, ALU.add).then_inc(var, 1)
                wait(pool, var, n + 1)
                nc.gpsimd.tensor_tensor(rms[:, c:c + 1], rms[:, 2 + c:3 + c], half[:, :], ALU.pow).then_inc(rms_ready, 1)

            def rotate(n, slot, turn, c, normed, part, rotated):
                heads = qk[:, c, :].rearrange("p (h d) -> p h d", d=HD)
                a = rot_a[:, :].rearrange("p (h d) -> p h d", d=HD)
                b = rot_b[:, :].rearrange("p (h d) -> p h d", d=HD)
                cos = cs[:, slot, 0:1, :].to_broadcast([P, NH, HD])
                sin = cs[:, slot, 1:2, :]
                wait(pool, x_loaded[slot], 32 * (turn + 1))
                wait(pool, normed, n + 1)
                nc.gpsimd.tensor_tensor(a, heads, cos, ALU.mult).then_inc(part, 1)
                lo, hi = slice(0, HD // 2), slice(HD // 2, HD)
                nc.gpsimd.tensor_tensor(b[:, :, lo], heads[:, :, hi], sin[:, :, lo].to_broadcast([P, NH, HD // 2]), ALU.mult).then_inc(part, 1)
                nc.gpsimd.tensor_tensor(b[:, :, hi], heads[:, :, lo], sin[:, :, hi].to_broadcast([P, NH, HD // 2]), ALU.mult).then_inc(part, 1)
                wait(pool, part, 3 * (n + 1))
                nc.gpsimd.tensor_tensor(heads, a, b, ALU.add).then_inc(rotated, 1)

            def step(s, j, turn):
                a, slot, a_turn = s + 1, (j + 1) % RING, turn + (j + 1) // RING
                if has(a):
                    rms_of(a, 0, q_sq, q_var, q_rms)
                    if not (isinstance(a, int) and a == 0):
                        wait(pool, k_rot, a)
                    rotate(a, slot, a_turn, 0, q_normed, q_part, q_rot)
                    rms_of(a, 1, k_sq, k_var, k_rms)
                    wait(pool, q_rot, a + 1)
                    rotate(a, slot, a_turn, 1, k_normed, k_part, k_rot)
                if has(s - 1):
                    wait_apart(pool, mv_made, s, passed["pool"])
                    nc.gpsimd.tensor_scalar(rstd[:, 1:2], mv[:, 1:2], 1.0, LN_EPS, ALU.mult, ALU.add).then_inc(ln_var, 1)
                    wait(pool, ln_var, s)
                    nc.gpsimd.tensor_tensor(rstd[:, 0:1], rstd[:, 1:2], half[:, :], ALU.pow).then_inc(ln_rstd, 1)

            steps(pool, step)

        @block.scalar
        def _(act):
            for k in range(KT):
                wait(act, w_loaded[k], 16)
                nc.scalar.copy(wqkv_hi[:, k, :], wqkv_raw[:, k, :]).then_inc(w_hi_made, 1)
            wait(act, w_loaded[KT], 16)
            nc.scalar.copy(wo_hi[:, :, :], wo_raw).then_inc(w_hi_made, 1)

            def exps(s, j, g, pair):
                for h in (2 * pair, 2 * pair + 1):
                    head = 4 * g + h
                    wait(act, masked, NH * s + head + 1)
                    p = prob[:, g % 2, h, :]
                    nc.scalar.activation(p, p, ACT.Exp, bias=nbias[:, j % 2, head:head + 1], scale=-1.0,
                                         accum_out=rsum[:, j % 2, head:head + 1]).then_inc(exp_made, 1)

            def probT_out(G):
                wait(act, probT_mm, 2 * G + 2)
                nc.scalar.copy(probT_at[0], probT_ps[:, :, 0:WB * P]).then_inc(probT_act, 1)

            probT_at = [None]

            def step(s, j, turn):
                a = s + 1
                for g in range(GROUPS):
                    probT_at[0] = probT[:, (g - 1) % 2, 2:4, :]
                    if g == 1 and has(s - 2):
                        wait(act, x1T_mm, s - 1)
                        nc.scalar.copy(x1T[:, :, bass.ts(s - 2, P)], ps_k[:, 0, :].rearrange("p (k t) -> p k t", k=KT)).then_inc(x1T_made, 1)
                    if g == 0 and has(a):
                        wait(act, xT_mm, a + 1)
                        nc.scalar.copy(xT_hi[:, :, :], ps_q[:, 0, :].rearrange("p (k t) -> p k t", k=KT)).then_inc(xT_hi_made, 1)
                    if g == 1 and has(a):
                        wait(act, q_mm, a + 1)
                        nc.scalar.activation(junk[:, 0, :], ps_q[:, 0, :], ACT.Square, accum_out=ssq[:, 0:1]).then_inc(q_sq, 1)
                    if has(s):
                        exps(s, j, g, 0)
                    if g == 3 and has(a):
                        wait(act, qT_mm, a + 1)
                        nc.scalar.copy(qT_hi[:, (j + 1) % 2, :, :], ps_q[:, 0, :].rearrange("p (k t) -> p k t", k=KT)).then_inc(qT_hi_made, 1)
                    if has(s) if g else has(s - 1):
                        probT_out(4 * s + g - 1)
                    if g == 0 and has(s - 1):
                        wait(act, rinvT_mm, s)
                        nc.scalar.copy(rinvT[:, :], ps_v[0:NH, 0, 0:P]).then_inc(rinvT_made, 1)
                    if g == 3 and has(a):
                        wait(act, kT_mm, a + 1)
                        nc.scalar.copy(kT_hi[:, :, (j + 1) % RING, :], ps_k[:, 0, :].rearrange("p (k t) -> p k t", k=KT)).then_inc(kT_hi_made, 1)
                    if g == 1 and has(a):
                        wait(act, k_mm, a + 1)
                        wait(act, q_sq, a + 1)
                        nc.scalar.activation(junk[:, 0, :], ps_k[:, 0, :], ACT.Square, accum_out=ssq[:, 1:2]).then_inc(k_sq, 1)
                    if has(s):
                        exps(s, j, g, 1)
                    if g == 0 and has(s - 1):
                        wait(act, rrep_mm, s)
                        nc.scalar.copy(r_rep[:, :], ps_v[:, 0, :]).then_inc(rrep_made, 1)
                    if g == 1:
                        if has(s - 1):
                            wait(act, oT_made, s)
                            nc.scalar.copy(oT_hi[:, :, :], oT[:, :].rearrange("p (k t) -> p k t", k=KT)).then_inc(oT_hi_made, 1)
                        if has(a):
                            wait(act, v_mm, a + 1)
                            wait(act, pv_mm, 4 * s)
                            if isinstance(s, int) and s < 3:
                                wait(act, cleared, 4)
                            nc.scalar.copy(v_ring[:, (j + 1) % RING, :], ps_v[:, 0, :]).then_inc(v_made, 1)

            steps(act, step)

        @block.vector
        def _(dve):
            for k in range(KT):
                wait(dve, w_hi_made, k + 1)
                nc.vector.tensor_tensor(wqkv_lo[:, k, :], wqkv_raw[:, k, :], wqkv_hi[:, k, :].bitcast(FP32), ALU.subtract).then_inc(w_lo_made, 1)
            wait(dve, w_hi_made, KT + 1)
            nc.vector.tensor_tensor(wo_lo[:, :, :], wo_raw, wo_hi[:, :, :].bitcast(FP32), ALU.subtract).then_inc(w_lo_made, 1)
            wait(dve, const_loaded, 16 * 5)

            def tiled(ap):
                return ap.rearrange("p (k t) -> p k t", k=KT)

            def masked_scores(s, j, g, pair):
                m = {0: 0, 1: 1}.get(s, 2) if isinstance(s, int) else 2
                for h in (2 * pair, 2 * pair + 1):
                    head = 4 * g + h
                    wait_apart(dve, score_mm, NH * s + head + 1, passed["dve"])
                    nc.vector.tensor_tensor_reduce(
                        out=prob[:, g % 2, h, :], in0=score_ps[h % 2][:, 0, 0:WB * P], in1=masks[:, m, :],
                        scale=-SCALE, scalar=3e38, op0=ALU.add, op1=ALU.min,
                        accum_out=nbias[:, j % 2, head:head + 1]).then_inc(masked, 1)

            def step(s, j, turn):
                a = s + 1
                for g in range(GROUPS):
                    if has(s) if g else has(s - 1):
                        G = 4 * s + g - 1
                        wait(dve, probT_mm, 2 * G + 1)
                        nc.vector.tensor_copy(probT[:, (g - 1) % 2, 0:2, :], probT_ps[:, :, 0:WB * P]).then_inc(probT_dve, 1)
                    if g == 0 and has(s - 1):
                        wait(dve, exp_made, NH * s)
                        nc.vector.reciprocal(rinv[:, :], rsum[:, (j - 1) % 2, :]).then_inc(rinv_made, 1)
                    if has(s):
                        masked_scores(s, j, g, 0)
                    if g == 0 and has(a):
                        wait(dve, xT_hi_made, a + 1)
                        nc.vector.tensor_tensor(xT_lo[:, :, :], tiled(ps_q[:, 0, :]), xT_hi[:, :, :].bitcast(FP32), ALU.subtract).then_inc(xT_lo_made, 1)
                    if g == 0 and has(s - 2):
                        wait(dve, ln_rstd, s - 1)
                        if isinstance(s, int) and s > NB - 2:
                            wait(dve, x1_stored, 16 * (s - 3))
                        nc.vector.tensor_scalar(x1[:, j % 2, :], res[:, :], mv[:, 0:1], rstd[:, 0:1], ALU.subtract, ALU.mult).then_inc(x1_made, 1)
                    if g == 3 and has(s - 1):
                        wait(dve, wo_mm, s)
                        wait(dve, x1_made, s - 1)
                        nc.vector.tensor_tensor(res[:, :], ps_v[:, 0, :], x_in[:, (j - 1) % RING, :], ALU.add).then_inc(res_made, 1)
                        wait(dve, res_made, s)
                        nc.vector.bn_stats(bn6[:, :], res[:, :]).then_inc(bn_made, 1)
                        wait_apart(dve, bn_made, s, passed["dve"])
                        nc.vector.bn_aggr(mv[:, :], bn6[:, :]).then_inc(mv_made, 1)
                    if g == 1 and has(a):
                        wait(dve, q_rms, a + 1)
                        nc.vector.scalar_tensor_tensor(qk[:, 0, :], ps_q[:, 0, :], rms[:, 0:1], qw_b[:, :], ALU.mult, ALU.mult).then_inc(q_normed, 1)
                    if g == 3 and has(a):
                        wait(dve, qT_hi_made, a + 1)
                        nc.vector.tensor_tensor(qT_lo[:, (j + 1) % 2, :, :], tiled(ps_q[:, 0, :]), qT_hi[:, (j + 1) % 2, :, :].bitcast(FP32), ALU.subtract).then_inc(qT_lo_made, 1)
                    if g == 3 and has(a):
                        wait(dve, kT_hi_made, a + 1)
                        nc.vector.tensor_tensor(kT_lo[:, :, (j + 1) % RING, :], tiled(ps_k[:, 0, :]), kT_hi[:, :, (j + 1) % RING, :].bitcast(FP32), ALU.subtract).then_inc(kT_lo_made, 1)
                    if has(s):
                        masked_scores(s, j, g, 1)
                    if g == 1 and has(a):
                        wait(dve, k_rms, a + 1)
                        nc.vector.scalar_tensor_tensor(qk[:, 1, :], ps_k[:, 0, :], rms[:, 1:2], kw_b[:, :], ALU.mult, ALU.mult).then_inc(k_normed, 1)
                    if g == 1 and has(s - 1):
                        wait(dve, pv_mm, 4 * s)
                        wait(dve, rrep_made, s)
                        wait(dve, oT_hi_made, s - 1)
                        nc.vector.tensor_tensor(oT[:, :], oT_ps[:, 0, :], r_rep[:, :], ALU.mult).then_inc(oT_made, 1)
                        wait(dve, oT_hi_made, s)
                        nc.vector.tensor_tensor(oT_lo[:, :, :], tiled(oT[:, :]), oT_hi[:, :, :].bitcast(FP32), ALU.subtract).then_inc(oT_lo_made, 1)

            steps(dve, step)

        @block.tensor
        def _(pe):
            def three(out, pairs):
                n = len(pairs)
                for i, (l, r) in enumerate(pairs):
                    last = nc.tensor.matmul(out, l, r, start=(i == 0), stop=(i == n - 1))
                return last

            def project(out, l_hi, l_lo, w_hi, w_lo, c):
                cols = slice(c * H, (c + 1) * H)
                return three(out, [p for k in range(KT) for p in (
                    (l_hi[:, k, :], w_lo[:, k, cols]), (l_hi[:, k, :], w_hi[:, k, cols]), (l_lo[:, k, :], w_hi[:, k, cols]))])

            def transposed(out, src):
                for k in range(KT):
                    last = nc.tensor.transpose(out[:, 0, k * P:(k + 1) * P], src[:, k * P:(k + 1) * P], ident[:, :])
                return last

            def scores(s, j, g, pair):
                for h in (2 * pair, 2 * pair + 1):
                    wait(pe, masked, NH * s + 4 * g + h - 1)
                    rows = slice(HD * h, HD * h + HD)
                    q_hi, q_lo = qT_hi[rows, j % 2, g, :], qT_lo[rows, j % 2, g, :]
                    for w, slot, n in window_runs(j)[0]:
                        out = score_ps[h % 2][:, 0, w * P:(w + n) * P]
                        k_hi, k_lo = kT_hi[rows, g, slot:slot + n, :], kT_lo[rows, g, slot:slot + n, :]
                        last = three(out, [(q_hi, k_lo), (q_hi, k_hi), (q_lo, k_hi)])
                    last.then_inc(score_mm, 1)

            def prob_transposes(G, g, pair):
                wait(pe, exp_made, 4 * G + 2 * pair + 2)
                if pair == 0:
                    wait(pe, probT_act, G)
                else:
                    wait(pe, probT_dve, G + 1)
                for h in range(2):
                    for w in range(WB):
                        last = nc.tensor.transpose(probT_ps[:, h, w * P:(w + 1) * P],
                                                   prob[:, g % 2, 2 * pair + h, w * P:(w + 1) * P], ident[:, :])
                last.then_inc(probT_mm, 1)

            def values(s, j, g):
                G = 4 * s + g
                if g == 0:
                    wait(pe, oT_made, s)
                wait(pe, probT_act, G + 1)
                for w, slot in enumerate(window_runs(j)[1]):
                    for h in range(4):
                        head = 4 * g + h
                        last = nc.tensor.matmul(oT_ps[HD * h:HD * h + HD, 0, g * P:(g + 1) * P],
                                                v_ring[:, slot, head * HD:(head + 1) * HD],
                                                probT[:, g % 2, h, w * P:(w + 1) * P],
                                                start=(w == 0), stop=(w == WB - 1))
                last.then_inc(pv_mm, 1)

            wait(pe, const_loaded, 16 * 5)

            def step(s, j, turn):
                a = s + 1
                for g in range(GROUPS):
                    behind = has(s) if g else has(s - 1)
                    if behind:
                        prob_transposes(4 * s + g - 1, (g - 1) % 4, 0)
                    if g == 0 and has(a):
                        wait(pe, x_loaded[(j + 1) % RING], 32 * (turn + (j + 1) // RING + 1))
                        wait(pe, qT_lo_made, a)
                        transposed(ps_q, x_in[:, (j + 1) % RING, :]).then_inc(xT_mm, 1)
                    if g == 1 and has(a):
                        wait(pe, xT_lo_made, a + 1)
                        if isinstance(s, int) and s < 0:
                            wait(pe, w_lo_made, KT)
                        project(ps_q[:, 0, :], xT_hi, xT_lo, wqkv_hi, wqkv_lo, 0).then_inc(q_mm, 1)
                    if has(s):
                        if g == 0:
                            wait(pe, kT_lo_made, s + 1)
                            if isinstance(s, int) and s == 0:
                                wait(pe, cleared, 4)
                        scores(s, j, g, 0)
                    if g == 3 and has(a):
                        wait(pe, q_rot, a + 1)
                        transposed(ps_q, qk[:, 0, :]).then_inc(qT_mm, 1)
                    if behind:
                        prob_transposes(4 * s + g - 1, (g - 1) % 4, 1)
                    if g == 0 and has(s - 1):
                        wait(pe, rinv_made, s)
                        wait(pe, res_made, s - 1)
                        nc.tensor.transpose(ps_v[0:NH, 0, 0:P], rinv[:, :], ident[:, :]).then_inc(rinvT_mm, 1)
                    if g == 1 and has(a):
                        wait(pe, x1T_made, s - 1)
                        project(ps_k[:, 0, :], xT_hi, xT_lo, wqkv_hi, wqkv_lo, 1).then_inc(k_mm, 1)
                    if g == 3 and has(a):
                        wait(pe, k_rot, a + 1)
                        transposed(ps_k, qk[:, 1, :]).then_inc(kT_mm, 1)
                    if has(s):
                        scores(s, j, g, 1)
                    if g < 2 and has(s - 1):
                        values(s - 1, (j - 1) % RING, g + 2)
                    if g >= 2 and has(s):
                        values(s, j, g - 2)
                    if g == 0 and has(s - 2):
                        wait(pe, x1_made, s - 1)
                        wait(pe, kT_lo_made, s + 1 if has(s) else NB)
                        transposed(ps_k, x1[:, j % 2, :]).then_inc(x1T_mm, 1)
                    if g == 0 and has(s - 1):
                        wait(pe, rinvT_made, s)
                        for k in range(KT):
                            last = nc.tensor.matmul(ps_v[:, 0, k * P:(k + 1) * P], sel[:, k, :], rinvT[:, :], start=True, stop=True)
                        last.then_inc(rrep_mm, 1)
                    if g == 1 and has(a):
                        wait(pe, rrep_made, s)
                        project(ps_v[:, 0, :], xT_hi, xT_lo, wqkv_hi, wqkv_lo, 2).then_inc(v_mm, 1)
                    if g == 2 and has(s - 1):
                        wait(pe, oT_lo_made, s)
                        wait(pe, v_made, s + 2 if has(a) else NB)
                        if isinstance(s, int) and s == 1:
                            wait(pe, w_lo_made, KT + 1)
                        project(ps_v[:, 0, :], oT_hi, oT_lo, wo_hi, wo_lo, 0).then_inc(wo_mm, 1)

            steps(pe, step)


def constants():
    inv_freq = (np.float32(1.0) / np.float32(THETA) ** (np.arange(0, HD, 2, dtype=np.float32) / np.float32(HD))).astype(np.float32)
    freqs = np.arange(S, dtype=np.float32)[:, None] * inv_freq[None, :]
    cos, sin = np.cos(freqs), np.sin(freqs)
    trig = np.stack([np.concatenate([cos, cos], 1), np.concatenate([-sin, sin], 1)], 1).astype(np.float32)
    q, k = np.arange(P)[:, None], np.arange(WB * P)[None, :]
    d = q + (WB - 1) * P - k
    seen = (d >= 0) & (d < WINDOW)
    masks = np.stack([np.where(seen & (k >= first * P), 0.0, NEG) for first in (2, 1, 0)], 1).astype(np.float32)
    sel = np.zeros((NH, KT, P), np.float32)
    for h in range(NH):
        sel[h, h // 4, (h % 4) * HD:(h % 4 + 1) * HD] = 1.0
    return trig, np.eye(P, dtype=np.float32), masks, sel


def ffn_phase(nc, W_router_gate, Ws_gu, Ws_down, We_gu, We_down, ident_in, index_in, x1_dram, x1T, out):
    TN = 512
    NT = S // TN
    BT = TN // P
    UNITS = 3
    EXPERT_W = [P, P, I_MOE - 2 * P]
    SHARED_W = [[P] * 3] * 3 + [[P] * 2]
    NCH = E + len(SHARED_W)
    CW = UNITS * P
    HRING = 4

    with ExitStack() as ctx:
        def sb(name, shape, dt=FP32):
            return ctx.enter_context(nc.sbuf_tensor(name, shape, dt))

        def sem(name):
            return ctx.enter_context(nc.semaphore(name))

        x_hi, x_lo = sb("x_hi", [P, KT, S], FP32R), sb("x_lo", [P, KT, S], FP32R)
        gu_raw, wd_raw = sb("gu_raw", [P, KT, 2 * CW]), sb("wd_raw", [P, UNITS, H])
        gu_hi, gu_lo = sb("gu_hi", [P, 2, KT, 2 * CW], FP32R), sb("gu_lo", [P, 2, KT, 2 * CW], FP32R)
        wd_hi, wd_lo = sb("wd_hi", [P, UNITS, H], FP32R), sb("wd_lo", [P, UNITS, H], FP32R)
        h_hi, h_lo = sb("h_hi", [P, HRING, TN], FP32R), sb("h_lo", [P, HRING, TN], FP32R)
        work = sb("work", [P, 4, TN])
        r_raw = sb("r_raw", [P, KT, NR])
        r_hi, r_lo = sb("r_hi", [P, KT, P], FP32R), sb("r_lo", [P, KT, P], FP32R)
        ident2 = sb("ident2", [P, P])
        index8 = sb("index8", [P, E])
        logits = sb("logits", [P, NB, NR])
        top = sb("top", [P, NB, 8])
        top_at = sb("top_at", [P, NB, 8], mybir.dt.uint32)
        top_f = sb("top_f", [P, NB, TOP_K])
        hit = sb("hit", [P, TOP_K, NB, E])
        red = sb("red", [P, 2, NB])
        combine = sb("combine", [P, NR, NB])
        scale = sb("scale", [P, 2, NB])
        bn6, mv, rstd = sb("bn6_y", [P, 2, 6]), sb("mv_y", [P, 2, 2]), sb("rstd_y", [P, 2, 2])
        half = sb("half_y", [P, 1])
        y = x1T[:, :, :].rearrange("p k s -> p (k s)").rearrange("p (b n) -> p b n", n=H)

        def bank(name):
            return ctx.enter_context(nc.psum_tensor(name, [P, TN], FP32))

        gate_ps = [bank(f"gate_ps{i}") for i in range(2)]
        up_ps = [bank(f"up_ps{i}") for i in range(2)]
        down_ps = [bank(f"down_ps{i}") for i in range(BT)]

        gu_loaded, wd_loaded, y_loaded, small_loaded, stored = map(sem, ("gu_loaded", "wd_loaded", "y_loaded", "small_loaded", "stored"))
        x_hi_made, x_lo_made, r_hi_made, r_lo_made, r_cleared = map(sem, ("x_hi_made", "x_lo_made", "r_hi_made", "r_lo_made", "r_cleared"))
        gu_hi_made, gu_lo_made, wd_hi_made, wd_lo_made = map(sem, ("gu_hi_made", "gu_lo_made", "wd_hi_made", "wd_lo_made"))
        gate_mm, up_mm, down_mm, logitT_mm, logit_mm = map(sem, ("gate_mm", "up_mm", "down_mm", "logitT_mm", "logit_mm"))
        silu_made, h_made, h_hi_made, h_lo_made, y_added = map(sem, ("silu_made", "h_made", "h_hi_made", "h_lo_made", "y_added"))
        logitT_made, exp_made, route, scale_made = map(sem, ("logitT_made", "router_exp_made", "route", "scale_made"))
        y_bn, y_mv, y_var, y_rstd, y_normed, pool_ready = map(sem, ("y_bn", "y_mv", "y_var", "y_rstd", "y_normed", "pool_ready"))

        def widths(c):
            return SHARED_W[c - E] if isinstance(c, int) and c >= E else EXPERT_W

        def gu_width(c):
            return 2 * sum(widths(c)) if isinstance(c, int) and c >= E else 2 * CW

        def first(c, tt):
            return UNITS * NT * c + len(widths(c)) * tt

        def behind_down(c, tt, u):
            back = u - HRING
            n = 0
            while back < 0:
                n += 1
                cc, t2 = (c, tt - n) if tt - n >= 0 else (c - 1, tt - n + NT)
                back += len(widths(cc))
            return NT * c + tt - n + 1

        def chunks(engine, chunk):
            for c in range(2):
                chunk(c, c)
            with engine.Fori(1, E // 2) as i:
                for par in range(2):
                    chunk(2 * i + par, par)
            for c in range(E, NCH):
                chunk(c, c % 2)

        block = ctx.enter_context(nc.Block())

        @block.sync
        def _(sp):
            def load_gu(c):
                if isinstance(c, int) and c >= E:
                    w, s0 = P * len(widths(c)), (c - E) * CW
                    src = Ws_gu.rearrange("(k p) n -> p k n", p=P)
                    parts = [src[:, :, s0:s0 + w], src[:, :, I_SH + s0:I_SH + s0 + w]]
                else:
                    w = I_MOE
                    src = We_gu[bass.ds(c, 1), :, :].rearrange("e (k p) n -> p (e k) n", p=P)
                    parts = [src[:, :, 0:w], src[:, :, w:2 * w]]
                for i, part in enumerate(parts):
                    sp.dma_start(gu_raw[:, :, i * w:(i + 1) * w], part).then_inc(gu_loaded, 16)

            def load_wd(c):
                if isinstance(c, int) and c >= E:
                    n, src = len(widths(c)), Ws_down[(c - E) * CW:(c - E) * CW + P * len(widths(c)), :]
                    sp.dma_start(wd_raw[:, 0:2, :], src[0:2 * P, :].rearrange("(u p) n -> p u n", p=P)).then_inc(wd_loaded, 16)
                    if n == 3:
                        sp.dma_start(wd_raw[:, 2, :], src[2 * P:, :]).then_inc(wd_loaded, 16)
                else:
                    src = We_down[bass.ds(c, 1), :, :].rearrange("e r n -> (e r) n")
                    sp.dma_start(wd_raw[:, 0:2, :], src[0:2 * P, :].rearrange("(u p) n -> p u n", p=P)).then_inc(wd_loaded, 16)
                    sp.dma_start(wd_raw[0:EXPERT_W[2], 2, :], src[2 * P:I_MOE, :]).then_inc(wd_loaded, 16)

            sp.dma_start(r_raw[:, :, :], W_router_gate.rearrange("(k p) n -> p k n", p=P)).then_inc(small_loaded, 16)
            sp.dma_start(ident2[:, :], ident_in).then_inc(small_loaded, 16)
            sp.dma_start(index8[:, :], index_in).then_inc(small_loaded, 16)
            load_gu(0)
            load_wd(0)
            wait(sp, x_lo_made, NT)
            sp.dma_start(y, x1_dram.rearrange("(b p) n -> p b n", p=P)).then_inc(y_loaded, 16)

            def chunk(c, par):
                nxt = c + 1
                if isinstance(c, int) and c == NCH - 1:
                    return
                wait(sp, gu_lo_made, KT * (c + 1))
                load_gu(nxt)
                wait(sp, wd_lo_made, UNITS * (c + 1))
                load_wd(nxt)

            for c in range(1):
                chunk(c, c)
            with sp.Fori(0, E // 2 - 1) as i:
                for par in range(2):
                    chunk(2 * i + 1 + par, par)
            for c in range(E - 1, NCH):
                chunk(c, c % 2)

            out_v = out.rearrange("(b p) n -> b p n", p=P)
            for b in range(NB):
                wait(sp, y_normed, b + 1)
                sp.dma_start(out_v[b], y[:, b, :]).then_inc(stored, 16)
            sp.wait_ge(stored, 16 * NB)

        @block.gpsimd
        def _(pool):
            pool.memset(r_hi[:, :, :].bitcast(FP32), 0.0).then_inc(r_cleared, 1)
            pool.memset(r_lo[:, :, :].bitcast(FP32), 0.0).then_inc(r_cleared, 1)
            pool.memset(gu_raw[:, :, 2 * I_MOE:], 0.0).then_inc(r_cleared, 1)
            pool.memset(half[:, :], -0.5).then_inc(pool_ready, 1)
            pool.wait_ge(pool_ready, 1)
            for b in range(NB):
                pool.wait_ge(y_mv, b + 1)
                nc.gpsimd.tensor_scalar(rstd[:, b % 2, 1:2], mv[:, b % 2, 1:2], 1.0, LN_EPS, ALU.mult, ALU.add).then_inc(y_var, 1)
                pool.wait_ge(y_var, b + 1)
                nc.gpsimd.tensor_tensor(rstd[:, b % 2, 0:1], rstd[:, b % 2, 1:2], half[:, :], ALU.pow).then_inc(y_rstd, 1)

        @block.scalar
        def _(act):
            for tt in range(NT):
                cols = slice(tt * TN, (tt + 1) * TN)
                nc.scalar.copy(x_hi[:, :, cols], x1T[:, :, cols]).then_inc(x_hi_made, 1)
            act.wait_ge(small_loaded, 48)
            act.wait_ge(r_cleared, 3)
            nc.scalar.copy(r_hi[:, :, 0:NR], r_raw[:, :, :]).then_inc(r_hi_made, 1)

            def split_gu(c, ks):
                wait(act, gu_loaded, 32 * (c + 1))
                n = gu_width(c)
                par = split_par[0]
                for k in ks:
                    nc.scalar.copy(gu_hi[:, par, k, 0:n], gu_raw[:, k, 0:n]).then_inc(gu_hi_made, 1)

            def split_wd(c):
                wait(act, wd_loaded, 32 * (c + 1) if not (isinstance(c, int) and c == NCH - 1) else 32 * c + 16)
                wait(act, down_mm, BT * NT * c)
                for u, w in enumerate(widths(c)):
                    nc.scalar.copy(wd_hi[0:w, u, :], wd_raw[0:w, u, :]).then_inc(wd_hi_made, 1)

            split_par = [0]
            split_gu(0, range(KT))
            for tt in range(NT):
                act.wait_ge(logitT_mm, tt + 1)
                nc.scalar.copy(work[0:NR, tt, :], down_ps[tt][0:NR, :]).then_inc(logitT_made, 1)
            act.wait_ge(route, 3)
            nc.scalar.activation(logits[:, :, :], logits[:, :, :], ACT.Exp).then_inc(exp_made, 1)

            def chunk(c, par):
                for tt in range(NT):
                    for u, w in enumerate(widths(c)):
                        n, at = first(c, tt) + u, (first(0 if not isinstance(c, int) else c, tt) + u)
                        wait(act, gate_mm, n + 1)
                        wait(act, h_made, n - 1)
                        if isinstance(c, int) and n < 2:
                            act.wait_ge(logit_mm, 1)
                        nc.scalar.activation(work[0:w, at % 2, :], gate_ps[at % 2][0:w, :], ACT.Silu).then_inc(silu_made, 1)
                        wait(act, h_made, n + 1)
                        turns = behind_down(c, tt, u)
                        wait(act, down_mm, BT * turns)
                        nc.scalar.copy(h_hi[0:w, at % HRING, :], work[0:w, 2 + at % 2, :]).then_inc(h_hi_made, 1)
                        if tt == 0 and u == 1:
                            split_wd(c)
                    if tt >= 1 and not (isinstance(c, int) and c == NCH - 1):
                        split_par[0] = 1 - par
                        split_gu(c + 1, {1: (0, 1), 2: (2,), 3: (3,)}[tt])

            chunks(act, chunk)

        @block.vector
        def _(dve):
            for tt in range(NT):
                cols = slice(tt * TN, (tt + 1) * TN)
                dve.wait_ge(x_hi_made, tt + 1)
                nc.vector.tensor_tensor(x_lo[:, :, cols], x1T[:, :, cols], x_hi[:, :, cols].bitcast(FP32), ALU.subtract).then_inc(x_lo_made, 1)
            dve.wait_ge(r_hi_made, 1)
            nc.vector.tensor_tensor(r_lo[:, :, 0:NR], r_raw[:, :, :], r_hi[:, :, 0:NR].bitcast(FP32), ALU.subtract).then_inc(r_lo_made, 1)

            def split_gu(c, par, ks):
                n = gu_width(c)
                for k in ks:
                    wait(dve, gu_hi_made, KT * c + k + 1)
                    nc.vector.tensor_tensor(gu_lo[:, par, k, 0:n], gu_raw[:, k, 0:n], gu_hi[:, par, k, 0:n].bitcast(FP32), ALU.subtract).then_inc(gu_lo_made, 1)

            def split_wd(c):
                for u, w in enumerate(widths(c)):
                    wait(dve, wd_hi_made, UNITS * c + u + 1)
                    nc.vector.tensor_tensor(wd_lo[0:w, u, :], wd_raw[0:w, u, :], wd_hi[0:w, u, :].bitcast(FP32), ALU.subtract).then_inc(wd_lo_made, 1)

            split_gu(0, 0, range(KT))

            steps_done = [0]

            def link(instruction):
                steps_done[0] += 1
                instruction.then_inc(route, 1)
                dve.wait_ge(route, steps_done[0])

            dve.wait_ge(logit_mm, 1)
            link(nc.vector.tensor_copy(logits[:, :, :], gate_ps[0][:, 0:NB * 16].rearrange("p (b n) -> p b n", n=16)[:, :, 0:NR]))
            link(nc.vector.tensor_reduce(red[:, 0, :], logits[:, :, 0:E], mybir.AxisListType.X, ALU.max))
            nc.vector.tensor_scalar(logits[:, :, E], logits[:, :, E], -1.0, None, ALU.mult)
            link(nc.vector.tensor_tensor(logits[:, :, 0:E], logits[:, :, 0:E], red[:, 0, :].unsqueeze(2).to_broadcast([P, NB, E]), ALU.subtract))
            dve.wait_ge(exp_made, 1)
            link(nc.vector.tensor_reduce(red[:, 0, :], logits[:, :, 0:E], mybir.AxisListType.X, ALU.add))
            link(nc.vector.reciprocal(red[:, 1, :], red[:, 0, :]))
            link(nc.vector.tensor_tensor(logits[:, :, 0:E], logits[:, :, 0:E], red[:, 1, :].unsqueeze(2).to_broadcast([P, NB, E]), ALU.mult))
            link(nc.vector.tensor_scalar(red[:, 0, :], logits[:, :, E], 1.0, None, ALU.add))
            nc.vector.reciprocal(combine[:, E, :], red[:, 0, :])
            for b in range(NB):
                last = nc.vector.max(top[:, b, :], logits[:, b, 0:E])
            link(last)
            for b in range(NB):
                last = nc.vector.max_index(top_at[:, b, :], top[:, b, :], logits[:, b, 0:E])
            link(last)
            link(nc.vector.tensor_copy(top_f[:, :, :], top_at[:, :, 0:TOP_K]))
            for t in range(TOP_K):
                last = nc.vector.tensor_tensor(hit[:, t, :, :], top_f[:, :, t:t + 1].to_broadcast([P, NB, E]),
                                               index8[:, :].unsqueeze(1).to_broadcast([P, NB, E]), ALU.is_equal)
            link(last)
            link(nc.vector.tensor_tensor(hit[:, 0, :, :], hit[:, 0, :, :], hit[:, 1, :, :], ALU.add))
            link(nc.vector.tensor_tensor(combine[:, 0:E, :].rearrange("p e b -> p b e"), logits[:, :, 0:E], hit[:, 0, :, :], ALU.mult))

            def add_down(c, par, tt):
                turn = NT * c + tt
                for i in range(BT):
                    b = BT * tt + i
                    wait(dve, down_mm, BT * turn + i + 1)
                    if isinstance(c, int) and c == 0 and tt == 0:
                        dve.wait_ge(y_loaded, 16)
                    if i == 0:
                        wait(dve, y_added, BT * (turn - NT + 1))
                        wait(dve, scale_made, c + 1)
                    nc.vector.scalar_tensor_tensor(y[:, b, :], down_ps[i][:, :], scale[:, par, b:b + 1], y[:, b, :], ALU.mult, ALU.add).then_inc(y_added, 1)

            def normalise(b):
                dve.wait_ge(y_added, BT * NT * (NCH - 1) + b + 1)
                nc.vector.bn_stats(bn6[:, b % 2, :], y[:, b, :]).then_inc(y_bn, 1)
                dve.wait_ge(y_bn, b + 1)
                nc.vector.bn_aggr(mv[:, b % 2, :], bn6[:, b % 2, :]).then_inc(y_mv, 1)

            def finish(b):
                dve.wait_ge(y_mv, b + 1)
                dve.wait_ge(y_rstd, b + 1)
                nc.vector.tensor_scalar(y[:, b, :], y[:, b, :], mv[:, b % 2, 0:1], rstd[:, b % 2, 0:1], ALU.subtract, ALU.mult).then_inc(y_normed, 1)

            def chunk(c, par):
                last_chunk = isinstance(c, int) and c == NCH - 1
                for tt in range(NT):
                    if tt == 0:
                        e = E if isinstance(c, int) and c >= E else c
                        nc.vector.tensor_copy(scale[:, par, :], combine[:, bass.ds(e, 1), :].rearrange("p e b -> p (e b)")).then_inc(scale_made, 1)
                    for u, w in enumerate(widths(c)):
                        n, at = first(c, tt) + u, (first(0 if not isinstance(c, int) else c, tt) + u)
                        wait(dve, silu_made, n + 1)
                        wait(dve, up_mm, n + 1)
                        wait(dve, h_lo_made, n - 1)
                        nc.vector.tensor_tensor(work[0:w, 2 + at % 2, :], work[0:w, at % 2, :], up_ps[at % 2][0:w, :], ALU.mult).then_inc(h_made, 1)
                        wait(dve, h_hi_made, n + 1)
                        nc.vector.tensor_tensor(h_lo[0:w, at % HRING, :], work[0:w, 2 + at % 2, :], h_hi[0:w, at % HRING, :].bitcast(FP32), ALU.subtract).then_inc(h_lo_made, 1)
                        if u == 0 and tt:
                            add_down(c, par, tt - 1)
                            if last_chunk:
                                for b in range(BT * (tt - 1), BT * tt):
                                    normalise(b)
                                    if b % 2:
                                        finish(b - 1)
                                        finish(b)
                        elif u == 0 and not (isinstance(c, int) and c == 0):
                            add_down(c - 1, 1 - par, NT - 1)
                        if u == 1 and tt == 0:
                            split_wd(c)
                    if tt >= 1 and not last_chunk:
                        split_gu(c + 1, 1 - par, {1: (0, 1), 2: (2,), 3: (3,)}[tt])

            chunks(dve, chunk)
            for i in range(BT):
                b = BT * (NT - 1) + i
                turn = NT * NCH - 1
                dve.wait_ge(down_mm, BT * turn + i + 1)
                nc.vector.scalar_tensor_tensor(y[:, b, :], down_ps[i][:, :], scale[:, (NCH - 1) % 2, b:b + 1], y[:, b, :], ALU.mult, ALU.add).then_inc(y_added, 1)
                normalise(b)
                if i:
                    finish(b - 1)
            finish(NB - 1)

        @block.tensor
        def _(pe):
            pe.wait_ge(small_loaded, 48)
            pe.wait_ge(r_lo_made, 1)
            for tt in range(NT):
                pe.wait_ge(x_lo_made, tt + 1)
                cols = slice(tt * TN, (tt + 1) * TN)
                for k in range(KT):
                    nc.tensor.matmul(down_ps[tt][:, :], r_lo[:, k, :], x_hi[:, k, cols], start=(k == 0), stop=False)
                    nc.tensor.matmul(down_ps[tt][:, :], r_hi[:, k, :], x_lo[:, k, cols], start=False, stop=False)
                    last = nc.tensor.matmul(down_ps[tt][:, :], r_hi[:, k, :], x_hi[:, k, cols], start=False, stop=(k == KT - 1))
                last.then_inc(logitT_mm, 1)
            for b in range(NB):
                pe.wait_ge(logitT_made, b // BT + 1)
                last = nc.tensor.transpose(gate_ps[0][:, 16 * b:16 * b + NR], work[0:NR, b // BT, (b % BT) * P:(b % BT + 1) * P], ident2[0:NR, 0:NR])
            last.then_inc(logit_mm, 1)
            pe.wait_ge(route, 1)

            def gate_up(c, par, tt, u):
                w, wsum = widths(c)[u], sum(widths(c))
                n, at = first(c, tt) + u, (first(0 if not isinstance(c, int) else c, tt) + u)
                cols = slice(tt * TN, (tt + 1) * TN)
                wait(pe, h_made, n - 1)
                for ps, base, done in ((gate_ps, 0, gate_mm), (up_ps, wsum, up_mm)):
                    o = ps[at % 2][0:w, :]
                    for k in range(KT):
                        if tt == 0 and u == 0 and base == 0:
                            wait(pe, gu_lo_made, KT * c + k + 1)
                        part = slice(base + u * P, base + u * P + w)
                        nc.tensor.matmul(o, gu_lo[:, par, k, part], x_hi[:, k, cols], start=(k == 0), stop=False)
                        nc.tensor.matmul(o, gu_hi[:, par, k, part], x_lo[:, k, cols], start=False, stop=False)
                        last = nc.tensor.matmul(o, gu_hi[:, par, k, part], x_hi[:, k, cols], start=False, stop=(k == KT - 1))
                    last.then_inc(done, 1)

            def down(c, tt):
                ws = widths(c)
                n, at = first(c, tt), first(0 if not isinstance(c, int) else c, tt)
                turn = NT * c + tt
                wait(pe, h_lo_made, n + len(ws))
                if tt == 0:
                    wait(pe, wd_lo_made, UNITS * c + len(ws))
                for i in range(BT):
                    wait(pe, y_added, BT * (turn - 1) + i + 1)
                    tok = slice(i * P, (i + 1) * P)
                    for u, w in enumerate(ws):
                        hh, hl = h_hi[0:w, (at + u) % HRING, tok], h_lo[0:w, (at + u) % HRING, tok]
                        nc.tensor.matmul(down_ps[i][:, :], hl, wd_hi[0:w, u, :], start=(u == 0), stop=False)
                        nc.tensor.matmul(down_ps[i][:, :], hh, wd_lo[0:w, u, :], start=False, stop=False)
                        last = nc.tensor.matmul(down_ps[i][:, :], hh, wd_hi[0:w, u, :], start=False, stop=(u == len(ws) - 1))
                    last.then_inc(down_mm, 1)

            def chunk(c, par):
                for tt in range(NT):
                    for u in range(len(widths(c))):
                        gate_up(c, par, tt, u)
                        if u == 0 and tt:
                            down(c, tt - 1)
                        elif u == 0 and not (isinstance(c, int) and c == 0):
                            down(c - 1, NT - 1)

            chunks(pe, chunk)
            down(NCH - 1, NT - 1)




def kernel(L0_attn_hidden_states, L0_attn_Wqkv, L0_attn_q_norm_w, L0_attn_k_norm_w, L0_attn_Wo,
           L0_ffn_W_router, L0_ffn_W_sgate, L0_ffn_Ws_gate_up, L0_ffn_Ws_down, L0_ffn_We_gate_up, L0_ffn_We_down):
    import concourse.bacc as bacc
    from concourse.bass_utils import run_bass_kernel_spmd

    trig, ident, masks, sel = constants()
    nc = bacc.Bacc("TRN2", target_bir_lowering=False, num_devices=1)
    arrays = {
        "x": np.asarray(L0_attn_hidden_states).reshape(S, H),
        "Wqkv": L0_attn_Wqkv, "q_w": L0_attn_q_norm_w, "k_w": L0_attn_k_norm_w, "Wo": L0_attn_Wo,
        "W_router_gate": np.concatenate([np.asarray(L0_ffn_W_router), np.asarray(L0_ffn_W_sgate)], 0).T,
        "Ws_gu": L0_ffn_Ws_gate_up, "Ws_down": L0_ffn_Ws_down, "We_gu": L0_ffn_We_gate_up, "We_down": L0_ffn_We_down,
        "trig": trig, "ident_c": ident, "masks_c": masks, "sel_c": sel,
        "index_c": np.tile(np.arange(E, dtype=np.float32), (P, 1)),
    }
    arrays = {f"in_{n}": np.ascontiguousarray(a) for n, a in arrays.items()}
    a = {n[3:]: nc.dram_tensor(n, v.shape, mybir.dt.from_np(v.dtype), kind="ExternalInput").ap() for n, v in arrays.items()}
    out = nc.dram_tensor("out_dram", (S, H), FP32, kind="ExternalOutput").ap()
    x1_dram = nc.dram_tensor("x1_dram", (S, H), FP32, kind="Internal").ap()
    with nc.sbuf_tensor("x1T", [P, KT, S], FP32) as x1T:
        attention_phase(nc, a["x"], a["Wqkv"], a["q_w"], a["k_w"], a["Wo"], a["trig"], a["ident_c"], a["masks_c"], a["sel_c"], x1_dram, x1T)
        ffn_phase(nc, a["W_router_gate"], a["Ws_gu"], a["Ws_down"], a["We_gu"], a["We_down"], a["ident_c"], a["index_c"], x1_dram, x1T, out)
    r = run_bass_kernel_spmd(nc, [arrays], core_ids=[0])
    return r.results[0]["out_dram"].reshape(1, S, H)
```

```python
import numpy as np
import concourse.bass as bass
from concourse import mybir
from contextlib import ExitStack

FP32 = mybir.dt.float32
FP32R = mybir.dt.float32r
ALU = mybir.AluOpType
ACT = mybir.ActivationFunctionType

P = 128
S = 2048
H = 512
NH, HD = 16, 32
KT = H // P
NB = S // P
WINDOW = 256
WB = WINDOW // P + 1
RING = 4
GROUPS = NH // 4
SCALE = 1.0 / HD ** 0.5
RMS_EPS, LN_EPS = 1e-6, 1e-5
NEG = -1e30
THETA = 10000.0

E, TOP_K, I_MOE, I_SH = 8, 2, 352, 1408
NR = E + 1


def wait(engine, semaphore, value):
    if isinstance(value, int) and value <= 0:
        return
    engine.wait_ge(semaphore, value)


def wait_apart(engine, semaphore, value, passed):
    wait(engine, semaphore, value)
    if not isinstance(value, int):
        engine.sem_inc(passed, 1)


UNITS = 3
CW = UNITS * P
GU_LOADS = 4


def pieces(c, Ws_gu, Ws_down, We_gu, We_down):
    found = []
    at, end = c * CW, (c + 1) * CW
    while at < end:
        if at < I_SH:
            gu, dn, n_in, col = Ws_gu, Ws_down, I_SH, at
        else:
            e, col = divmod(at - I_SH, I_MOE)
            gu, dn, n_in = We_gu[e], We_down[e], I_MOE
        n = min(end - at, n_in - col)
        if n == CW:
            n = CW - P
        found.append((at - c * CW, n, gu, n_in, dn, col))
        at += n
    return found


def load_gu(sp, dst, parts, half, loaded):
    rows = slice(half * H // 2, (half + 1) * H // 2)
    for at, n, gu, up, _, col in parts:
        for base, src in ((0, col), (CW, up + col)):
            sp.dma_start(dst[:, :, base + at:base + at + n],
                         gu[rows, src:src + n].rearrange("(k p) n -> p k n", p=P)).then_inc(loaded, 16)


def window_runs(j):
    slots = [(j - WB + 1 + w) % RING for w in range(WB)]
    runs = []
    for w, slot in enumerate(slots):
        if runs and runs[-1][1] + runs[-1][2] == slot:
            runs[-1][2] += 1
        else:
            runs.append([w, slot, 1])
    return runs, slots


def attention_phase(nc, x, Wqkv, q_w, k_w, Wo, trig, ident_in, masks_in, x1_dram, x1T, load_ahead):
    with ExitStack() as ctx:
        def sb(name, shape, dt=FP32):
            return ctx.enter_context(nc.sbuf_tensor(name, shape, dt))

        def sem(name):
            return ctx.enter_context(nc.semaphore(name))

        ident = sb("ident", [P, P])
        masks = sb("masks", [P, 3, WB * P])
        qw_b, kw_b = sb("qw_b", [P, H]), sb("kw_b", [P, H])
        wqkv_hi, wqkv_lo = sb("wqkv_hi", [P, KT, 3 * H], FP32R), sb("wqkv_lo", [P, KT, 3 * H], FP32R)
        wo_hi, wo_lo = sb("wo_hi", [P, KT, H], FP32R), sb("wo_lo", [P, KT, H], FP32R)
        half = sb("half", [P, 1])
        x_in = sb("x_in", [P, RING, H])
        cs = sb("cs", [P, RING, 2, HD])
        xT_hi, xT_lo = sb("xT_hi", [P, KT, P], FP32R), sb("xT_lo", [P, KT, P], FP32R)
        qk = sb("qk", [P, 2, H])
        rot_a, rot_b = sb("rot_a", [P, H]), sb("rot_b", [P, H])
        scratch = sb("scratch", [P, H])
        ssq, rms = sb("ssq", [P, 2]), sb("rms", [P, 4])
        qT_hi, qT_lo = sb("qT_hi", [P, 2, KT, P], FP32R), sb("qT_lo", [P, 2, KT, P], FP32R)
        kT_hi, kT_lo = sb("kT_hi", [P, KT, RING, P], FP32R), sb("kT_lo", [P, KT, RING, P], FP32R)
        v_ring = sb("v_ring", [P, RING, H])
        prob = sb("prob", [P, 2, 4, WB * P])
        probT = sb("probT", [P, 2, 4, WB * P])
        nbias, rsum = sb("nbias", [P, 2, NH]), sb("rsum", [P, 2, NH])
        rinv = sb("rinv", [P, NH])
        r_rep = sb("r_rep", [P, H])
        oT = sb("oT", [P, H])
        oT_hi, oT_lo = sb("oT_hi", [P, KT, P], FP32R), sb("oT_lo", [P, KT, P], FP32R)
        res = sb("res", [P, H])
        bn6, mv, rstd = sb("bn6", [P, 6]), sb("mv", [P, 2]), sb("rstd", [P, 2])
        x1 = sb("x1", [P, 2, H])

        def bank(name, n=1):
            return ctx.enter_context(nc.psum_tensor(name, [P, n, H], FP32))

        score_ps = [bank(f"score_ps{i}") for i in range(2)]
        probT_ps = bank("probT_ps", 2)
        oT_ps = bank("oT_ps")
        ps_q, ps_k, ps_v = bank("ps_q"), bank("ps_k"), bank("ps_v")

        w_loaded = [sem(f"w_loaded_{part}") for part in "qkvo"]
        ident_loaded, const_loaded = sem("ident_loaded"), sem("const_loaded")
        x_loaded = [sem(f"x_loaded{i}") for i in range(RING)]
        x1_stored = sem("x1_stored")
        passed = {e: sem(f"{e}_waits_passed") for e in ("dve", "pool", "sp")}
        w_hi_made, w_lo_made, cleared = sem("w_hi_made"), sem("w_lo_made"), sem("cleared")
        xT_mm, q_mm, k_mm, v_mm, qT_mm, kT_mm = map(sem, ("xT_mm", "q_mm", "k_mm", "v_mm", "qT_mm", "kT_mm"))
        score_mm, probT_mm, pv_mm = map(sem, ("score_mm", "probT_mm", "pv_mm"))
        rrep_mm, wo_mm, x1T_mm = map(sem, ("rrep_mm", "wo_mm", "x1T_mm"))
        xT_hi_made, q_sq, k_sq, v_made, exp_made = map(sem, ("xT_hi_made", "q_sq", "k_sq", "v_made", "exp_made"))
        probT_act, rrep_made, oT_hi_made = map(sem, ("probT_act", "rrep_made", "oT_hi_made"))
        x1T_made, qT_hi_made, kT_hi_made = map(sem, ("x1T_made", "qT_hi_made", "kT_hi_made"))
        xT_lo_made, q_normed, k_normed, masked = map(sem, ("xT_lo_made", "q_normed", "k_normed", "masked"))
        probT_dve, rinv_made, rinv_spread, oT_made, oT_lo_made = map(sem, ("probT_dve", "rinv_made", "rinv_spread", "oT_made", "oT_lo_made"))
        res_made, bn_made, mv_made, x1_made = map(sem, ("res_made", "bn_made", "mv_made", "x1_made"))
        qT_lo_made, kT_lo_made = map(sem, ("qT_lo_made", "kT_lo_made"))
        q_var, k_var, q_rms, k_rms = map(sem, ("q_var", "k_var", "q_rms", "k_rms"))
        q_part, k_part, q_rot, k_rot = map(sem, ("q_part", "k_part", "q_rot", "k_rot"))
        ln_var, ln_rstd = map(sem, ("ln_var", "ln_rstd"))

        staged = x1T[:, :, :].rearrange("p k s -> p (k s)")
        wqkv_raw = staged[:, 0:KT * 3 * H].rearrange("p (k n) -> p k n", k=KT)
        wo_raw = staged[:, KT * 3 * H:].rearrange("p (k n) -> p k n", k=KT)

        def steps(engine, step):
            for s in (-1, 0, 1):
                step(s, s % RING, s // RING)
            with engine.Fori(0, 3) as i:
                for j in range(RING):
                    s0 = 2 + j
                    step(RING * i + s0, s0 % RING, i + s0 // RING)
            for s in range(14, 18):
                step(s, s % RING, s // RING)

        def has(block):
            return not isinstance(block, int) or 0 <= block < NB

        block = ctx.enter_context(nc.Block())

        @block.sync
        def _(sp):
            def load_x(n, slot):
                sp.dma_start(x_in[:, slot, :], x[bass.ts(n, P), :]).then_inc(x_loaded[slot], 16)
                sp.dma_start(cs[:, slot, :, :], trig[bass.ts(n, P), :, :]).then_inc(x_loaded[slot], 16)

            sp.dma_start(ident[:, :], ident_in).then_inc(ident_loaded, 16)
            load_x(0, 0)
            for c in range(3):
                sp.dma_start(wqkv_raw[:, :, c * H:(c + 1) * H], Wqkv[:, c * H:(c + 1) * H].rearrange("(k p) n -> p k n", p=P)).then_inc(w_loaded[c], 16)
            sp.dma_start(qw_b[:, :], q_w.partition_broadcast(P)).then_inc(const_loaded, 16)
            sp.dma_start(kw_b[:, :], k_w.partition_broadcast(P)).then_inc(const_loaded, 16)
            sp.dma_start(masks[:, :, :], masks_in).then_inc(const_loaded, 16)
            sp.dma_start(wo_raw, Wo.rearrange("(k p) n -> p k n", p=P)).then_inc(w_loaded[3], 16)
            load_x(1, 1)

            def step(s, j, turn):
                if isinstance(s, int) and s < 0:
                    return
                if isinstance(s, int) and s == 1:
                    load_ahead(sp)
                if has(s + 2):
                    wait(sp, res_made, s - 1)
                    wait(sp, k_rot, s - 1)
                    load_x(s + 2, (j + 2) % RING)
                if has(s - 2):
                    wait(sp, x1_made, s - 1)
                    sp.dma_start(x1_dram[bass.ts(s - 2, P), :], x1[:, j % 2, :]).then_inc(x1_stored, 16)
                    wait_apart(sp, x1_stored, 16 * (s - 1), passed["sp"])

            steps(sp, step)

        @block.gpsimd
        def _(pool):
            pool.memset(half[:, :], -0.5).then_inc(cleared, 1)
            pool.memset(v_ring[:, 2:4, :], 0.0).then_inc(cleared, 1)
            pool.memset(kT_hi[:, :, 2:4, :].bitcast(FP32), 0.0).then_inc(cleared, 1)
            pool.memset(kT_lo[:, :, 2:4, :].bitcast(FP32), 0.0).then_inc(cleared, 1)
            pool.wait_ge(cleared, 4)

            def rms_of(n, c, squares, var, rms_ready):
                wait_apart(pool, squares, n + 1, passed["pool"])
                nc.gpsimd.tensor_scalar(rms[:, 2 + c:3 + c], ssq[:, c:c + 1], 1.0 / H, RMS_EPS, ALU.mult, ALU.add).then_inc(var, 1)
                wait(pool, var, n + 1)
                nc.gpsimd.tensor_tensor(rms[:, c:c + 1], rms[:, 2 + c:3 + c], half[:, :], ALU.pow).then_inc(rms_ready, 1)

            def rotate(n, slot, turn, c, normed, part, rotated):
                heads = qk[:, c, :].rearrange("p (h d) -> p h d", d=HD)
                a = rot_a[:, :].rearrange("p (h d) -> p h d", d=HD)
                b = rot_b[:, :].rearrange("p (h d) -> p h d", d=HD)
                cos = cs[:, slot, 0:1, :].to_broadcast([P, NH, HD])
                sin = cs[:, slot, 1:2, :]
                wait(pool, x_loaded[slot], 32 * (turn + 1))
                wait(pool, normed, n + 1)
                nc.gpsimd.tensor_tensor(a, heads, cos, ALU.mult).then_inc(part, 1)
                lo, hi = slice(0, HD // 2), slice(HD // 2, HD)
                nc.gpsimd.tensor_tensor(b[:, :, lo], heads[:, :, hi], sin[:, :, lo].to_broadcast([P, NH, HD // 2]), ALU.mult).then_inc(part, 1)
                nc.gpsimd.tensor_tensor(b[:, :, hi], heads[:, :, lo], sin[:, :, hi].to_broadcast([P, NH, HD // 2]), ALU.mult).then_inc(part, 1)
                wait(pool, part, 3 * (n + 1))
                nc.gpsimd.tensor_tensor(heads, a, b, ALU.add).then_inc(rotated, 1)

            def step(s, j, turn):
                a, slot, a_turn = s + 1, (j + 1) % RING, turn + (j + 1) // RING
                if has(a):
                    rms_of(a, 0, q_sq, q_var, q_rms)
                    if not (isinstance(a, int) and a == 0):
                        wait(pool, k_rot, a)
                    rotate(a, slot, a_turn, 0, q_normed, q_part, q_rot)
                    rms_of(a, 1, k_sq, k_var, k_rms)
                    wait(pool, q_rot, a + 1)
                    rotate(a, slot, a_turn, 1, k_normed, k_part, k_rot)
                if has(s - 1):
                    wait_apart(pool, mv_made, s, passed["pool"])
                    nc.gpsimd.tensor_scalar(rstd[:, 1:2], mv[:, 1:2], 1.0, LN_EPS, ALU.mult, ALU.add).then_inc(ln_var, 1)
                    wait(pool, ln_var, s)
                    nc.gpsimd.tensor_tensor(rstd[:, 0:1], rstd[:, 1:2], half[:, :], ALU.pow).then_inc(ln_rstd, 1)

            steps(pool, step)

        @block.scalar
        def _(act):
            def split_wqkv(c):
                act.wait_ge(w_loaded[c], 16)
                for i in range(2):
                    part = (slice(None), slice(2 * i, 2 * i + 2), slice(c * H, (c + 1) * H))
                    nc.scalar.copy(wqkv_hi[part], wqkv_raw[part]).then_inc(w_hi_made, 1)

            def split_wo():
                act.wait_ge(w_loaded[3], 16)
                nc.scalar.copy(wo_hi[:, :, :], wo_raw).then_inc(w_hi_made, 1)

            def exps(s, j, g, pair):
                for h in (2 * pair, 2 * pair + 1):
                    head = 4 * g + h
                    wait(act, masked, NH * s + head + 1)
                    p = prob[:, g % 2, h, :]
                    nc.scalar.activation(p, p, ACT.Exp, bias=nbias[:, j % 2, head:head + 1], scale=-1.0,
                                         accum_out=rsum[:, j % 2, head:head + 1]).then_inc(exp_made, 1)

            def probT_out(G):
                wait(act, probT_mm, 2 * G + 2)
                nc.scalar.copy(probT_at[0], probT_ps[:, :, 0:WB * P]).then_inc(probT_act, 1)

            probT_at = [None]

            def step(s, j, turn):
                a = s + 1
                for g in range(GROUPS):
                    probT_at[0] = probT[:, (g - 1) % 2, 2:4, :]
                    if g == 1 and has(s - 2):
                        wait(act, x1T_mm, s - 1)
                        nc.scalar.copy(x1T[:, :, bass.ts(s - 2, P)], ps_k[:, 0, :].rearrange("p (k t) -> p k t", k=KT)).then_inc(x1T_made, 1)
                    if g == 0 and has(a):
                        wait(act, xT_mm, a + 1)
                        nc.scalar.copy(xT_hi[:, :, :], ps_q[:, 0, :].rearrange("p (k t) -> p k t", k=KT)).then_inc(xT_hi_made, 1)
                    if isinstance(s, int) and s == -1 and g == 0:
                        split_wqkv(0)
                        split_wqkv(1)
                    if isinstance(s, int) and s == -1 and g == 3:
                        split_wo()
                    if g == 1 and has(a):
                        wait(act, q_mm, a + 1)
                        nc.scalar.activation(scratch[:, :], ps_q[:, 0, :], ACT.Square, accum_out=ssq[:, 0:1]).then_inc(q_sq, 1)
                        if isinstance(s, int) and s == -1:
                            split_wqkv(2)
                    if has(s):
                        exps(s, j, g, 0)
                    if g == 3 and has(a):
                        wait(act, qT_mm, a + 1)
                        nc.scalar.copy(qT_hi[:, (j + 1) % 2, :, :], ps_q[:, 0, :].rearrange("p (k t) -> p k t", k=KT)).then_inc(qT_hi_made, 1)
                    if has(s) if g else has(s - 1):
                        probT_out(4 * s + g - 1)
                    if g == 3 and has(a):
                        wait(act, kT_mm, a + 1)
                        nc.scalar.copy(kT_hi[:, :, (j + 1) % RING, :], ps_k[:, 0, :].rearrange("p (k t) -> p k t", k=KT)).then_inc(kT_hi_made, 1)
                    if g == 1 and has(a):
                        wait(act, k_mm, a + 1)
                        wait(act, q_sq, a + 1)
                        nc.scalar.activation(scratch[:, :], ps_k[:, 0, :], ACT.Square, accum_out=ssq[:, 1:2]).then_inc(k_sq, 1)
                    if has(s):
                        exps(s, j, g, 1)
                    if g == 0 and has(s - 1):
                        wait(act, rrep_mm, s)
                        nc.scalar.copy(r_rep[:, :], ps_v[:, 0, :]).then_inc(rrep_made, 1)
                    if g == 1:
                        if has(s - 1):
                            wait(act, oT_made, s)
                            nc.scalar.copy(oT_hi[:, :, :], oT[:, :].rearrange("p (k t) -> p k t", k=KT)).then_inc(oT_hi_made, 1)
                        if has(a):
                            wait(act, v_mm, a + 1)
                            wait(act, pv_mm, 4 * s)
                            if isinstance(s, int) and s < 3:
                                wait(act, cleared, 4)
                            nc.scalar.copy(v_ring[:, (j + 1) % RING, :], ps_v[:, 0, :]).then_inc(v_made, 1)

            steps(act, step)

        @block.vector
        def _(dve):
            def split_wqkv():
                for n in range(6):
                    c, i = divmod(n, 2)
                    part = (slice(None), slice(2 * i, 2 * i + 2), slice(c * H, (c + 1) * H))
                    dve.wait_ge(w_hi_made, n + 1)
                    nc.vector.tensor_tensor(wqkv_lo[part], wqkv_raw[part], wqkv_hi[part].bitcast(FP32), ALU.subtract).then_inc(w_lo_made, 1)
                dve.wait_ge(const_loaded, 16 * 3)

            def split_wo():
                dve.wait_ge(w_hi_made, 7)
                nc.vector.tensor_tensor(wo_lo[:, :, :], wo_raw, wo_hi[:, :, :].bitcast(FP32), ALU.subtract).then_inc(w_lo_made, 1)

            def tiled(ap):
                return ap.rearrange("p (k t) -> p k t", k=KT)

            def masked_scores(s, j, g, pair):
                m = {0: 0, 1: 1}.get(s, 2) if isinstance(s, int) else 2
                for h in (2 * pair, 2 * pair + 1):
                    head = 4 * g + h
                    wait_apart(dve, score_mm, NH * s + head + 1, passed["dve"])
                    nc.vector.tensor_tensor_reduce(
                        out=prob[:, g % 2, h, :], in0=score_ps[h % 2][:, 0, 0:WB * P], in1=masks[:, m, :],
                        scale=-SCALE, scalar=3e38, op0=ALU.add, op1=ALU.min,
                        accum_out=nbias[:, j % 2, head:head + 1]).then_inc(masked, 1)

            def step(s, j, turn):
                a = s + 1
                for g in range(GROUPS):
                    if has(s) if g else has(s - 1):
                        G = 4 * s + g - 1
                        wait(dve, probT_mm, 2 * G + 1)
                        nc.vector.tensor_copy(probT[:, (g - 1) % 2, 0:2, :], probT_ps[:, :, 0:WB * P]).then_inc(probT_dve, 1)
                    if g == 0 and has(s - 1):
                        wait(dve, exp_made, NH * s)
                        nc.vector.reciprocal(rinv[:, :], rsum[:, (j - 1) % 2, :]).then_inc(rinv_made, 1)
                        wait(dve, rinv_made, s)
                        wait(dve, k_sq, s)
                        nc.vector.tensor_copy(scratch[:, :].rearrange("p (h d) -> p h d", d=HD), rinv[:, :].unsqueeze(2).to_broadcast([P, NH, HD])).then_inc(rinv_spread, 1)
                    if has(s):
                        masked_scores(s, j, g, 0)
                    if g == 0 and has(a):
                        wait(dve, xT_hi_made, a + 1)
                        nc.vector.tensor_tensor(xT_lo[:, :, :], tiled(ps_q[:, 0, :]), xT_hi[:, :, :].bitcast(FP32), ALU.subtract).then_inc(xT_lo_made, 1)
                    if isinstance(s, int) and s == -1 and g == 0:
                        split_wqkv()
                    if isinstance(s, int) and s == -1 and g == 3:
                        split_wo()
                    if g == 0 and has(s - 2):
                        wait(dve, ln_rstd, s - 1)
                        if isinstance(s, int) and s > NB - 2:
                            wait(dve, x1_stored, 16 * (s - 3))
                        nc.vector.tensor_scalar(x1[:, j % 2, :], res[:, :], mv[:, 0:1], rstd[:, 0:1], ALU.subtract, ALU.mult).then_inc(x1_made, 1)
                    if g == 3 and has(s - 1):
                        wait(dve, wo_mm, s)
                        wait(dve, x1_made, s - 1)
                        nc.vector.tensor_tensor(res[:, :], ps_v[:, 0, :], x_in[:, (j - 1) % RING, :], ALU.add).then_inc(res_made, 1)
                        wait(dve, res_made, s)
                        nc.vector.bn_stats(bn6[:, :], res[:, :]).then_inc(bn_made, 1)
                        wait_apart(dve, bn_made, s, passed["dve"])
                        nc.vector.bn_aggr(mv[:, :], bn6[:, :]).then_inc(mv_made, 1)
                    if g == 1 and has(a):
                        wait(dve, q_rms, a + 1)
                        nc.vector.scalar_tensor_tensor(qk[:, 0, :], ps_q[:, 0, :], rms[:, 0:1], qw_b[:, :], ALU.mult, ALU.mult).then_inc(q_normed, 1)
                    if g == 3 and has(a):
                        wait(dve, qT_hi_made, a + 1)
                        nc.vector.tensor_tensor(qT_lo[:, (j + 1) % 2, :, :], tiled(ps_q[:, 0, :]), qT_hi[:, (j + 1) % 2, :, :].bitcast(FP32), ALU.subtract).then_inc(qT_lo_made, 1)
                    if g == 3 and has(a):
                        wait(dve, kT_hi_made, a + 1)
                        nc.vector.tensor_tensor(kT_lo[:, :, (j + 1) % RING, :], tiled(ps_k[:, 0, :]), kT_hi[:, :, (j + 1) % RING, :].bitcast(FP32), ALU.subtract).then_inc(kT_lo_made, 1)
                    if has(s):
                        masked_scores(s, j, g, 1)
                    if g == 1 and has(a):
                        wait(dve, k_rms, a + 1)
                        nc.vector.scalar_tensor_tensor(qk[:, 1, :], ps_k[:, 0, :], rms[:, 1:2], kw_b[:, :], ALU.mult, ALU.mult).then_inc(k_normed, 1)
                    if g == 1 and has(s - 1):
                        wait(dve, pv_mm, 4 * s)
                        wait(dve, rrep_made, s)
                        wait(dve, oT_hi_made, s - 1)
                        nc.vector.tensor_tensor(oT[:, :], oT_ps[:, 0, :], r_rep[:, :], ALU.mult).then_inc(oT_made, 1)
                        wait(dve, oT_hi_made, s)
                        nc.vector.tensor_tensor(oT_lo[:, :, :], tiled(oT[:, :]), oT_hi[:, :, :].bitcast(FP32), ALU.subtract).then_inc(oT_lo_made, 1)

            steps(dve, step)

        @block.tensor
        def _(pe):
            def three(out, pairs):
                n = len(pairs)
                for i, (l, r) in enumerate(pairs):
                    last = nc.tensor.matmul(out, l, r, start=(i == 0), stop=(i == n - 1))
                return last

            def project(out, l_hi, l_lo, w_hi, w_lo, c, first=False):
                cols = slice(c * H, (c + 1) * H)
                if first:
                    for k in range(KT):
                        pe.wait_ge(w_lo_made, 2 * c + k // 2 + 1)
                        nc.tensor.matmul(out, l_hi[:, k, :], w_lo[:, k, cols], start=(k == 0), stop=False)
                        nc.tensor.matmul(out, l_hi[:, k, :], w_hi[:, k, cols], start=False, stop=False)
                        last = nc.tensor.matmul(out, l_lo[:, k, :], w_hi[:, k, cols], start=False, stop=(k == KT - 1))
                    return last
                return three(out, [p for k in range(KT) for p in (
                    (l_hi[:, k, :], w_lo[:, k, cols]), (l_hi[:, k, :], w_hi[:, k, cols]), (l_lo[:, k, :], w_hi[:, k, cols]))])

            def transposed(out, src):
                for k in range(KT):
                    last = nc.tensor.transpose(out[:, 0, k * P:(k + 1) * P], src[:, k * P:(k + 1) * P], ident[:, :])
                return last

            def scores(s, j, g, pair):
                for h in (2 * pair, 2 * pair + 1):
                    wait(pe, masked, NH * s + 4 * g + h - 1)
                    rows = slice(HD * h, HD * h + HD)
                    q_hi, q_lo = qT_hi[rows, j % 2, g, :], qT_lo[rows, j % 2, g, :]
                    for w, slot, n in window_runs(j)[0]:
                        out = score_ps[h % 2][:, 0, w * P:(w + n) * P]
                        k_hi, k_lo = kT_hi[rows, g, slot:slot + n, :], kT_lo[rows, g, slot:slot + n, :]
                        last = three(out, [(q_hi, k_lo), (q_hi, k_hi), (q_lo, k_hi)])
                    last.then_inc(score_mm, 1)

            def prob_transposes(G, g, pair):
                wait(pe, exp_made, 4 * G + 2 * pair + 2)
                if pair == 0:
                    wait(pe, probT_act, G)
                else:
                    wait(pe, probT_dve, G + 1)
                for h in range(2):
                    for w in range(WB):
                        last = nc.tensor.transpose(probT_ps[:, h, w * P:(w + 1) * P],
                                                   prob[:, g % 2, 2 * pair + h, w * P:(w + 1) * P], ident[:, :])
                last.then_inc(probT_mm, 1)

            def values(s, j, g):
                G = 4 * s + g
                if g == 0:
                    wait(pe, oT_made, s)
                wait(pe, probT_act, G + 1)
                for w, slot in enumerate(window_runs(j)[1]):
                    for h in range(4):
                        head = 4 * g + h
                        last = nc.tensor.matmul(oT_ps[HD * h:HD * h + HD, 0, g * P:(g + 1) * P],
                                                v_ring[:, slot, head * HD:(head + 1) * HD],
                                                probT[:, g % 2, h, w * P:(w + 1) * P],
                                                start=(w == 0), stop=(w == WB - 1))
                last.then_inc(pv_mm, 1)

            pe.wait_ge(ident_loaded, 16)

            def step(s, j, turn):
                a = s + 1
                for g in range(GROUPS):
                    behind = has(s) if g else has(s - 1)
                    is_first = isinstance(s, int) and s == -1
                    if behind:
                        prob_transposes(4 * s + g - 1, (g - 1) % 4, 0)
                    if g == 0 and has(a):
                        wait(pe, x_loaded[(j + 1) % RING], 32 * (turn + (j + 1) // RING + 1))
                        wait(pe, qT_lo_made, a)
                        transposed(ps_q, x_in[:, (j + 1) % RING, :]).then_inc(xT_mm, 1)
                    if g == 1 and has(a):
                        wait(pe, xT_lo_made, a + 1)
                        project(ps_q[:, 0, :], xT_hi, xT_lo, wqkv_hi, wqkv_lo, 0, is_first).then_inc(q_mm, 1)
                    if has(s):
                        if g == 0:
                            wait(pe, kT_lo_made, s + 1)
                            if isinstance(s, int) and s == 0:
                                wait(pe, cleared, 4)
                        scores(s, j, g, 0)
                    if g == 3 and has(a):
                        wait(pe, q_rot, a + 1)
                        transposed(ps_q, qk[:, 0, :]).then_inc(qT_mm, 1)
                    if behind:
                        prob_transposes(4 * s + g - 1, (g - 1) % 4, 1)
                    if g == 0 and has(s - 1):
                        wait(pe, rinv_spread, s)
                        wait(pe, res_made, s - 1)
                        for k in range(KT):
                            last = nc.tensor.transpose(ps_v[:, 0, k * P:(k + 1) * P], scratch[:, k * P:(k + 1) * P], ident[:, :])
                        last.then_inc(rrep_mm, 1)
                    if g == 1 and has(a):
                        wait(pe, x1T_made, s - 1)
                        project(ps_k[:, 0, :], xT_hi, xT_lo, wqkv_hi, wqkv_lo, 1, is_first).then_inc(k_mm, 1)
                    if g == 3 and has(a):
                        wait(pe, k_rot, a + 1)
                        transposed(ps_k, qk[:, 1, :]).then_inc(kT_mm, 1)
                    if has(s):
                        scores(s, j, g, 1)
                    if g < 2 and has(s - 1):
                        values(s - 1, (j - 1) % RING, g + 2)
                    if g >= 2 and has(s):
                        values(s, j, g - 2)
                    if g == 0 and has(s - 2):
                        wait(pe, x1_made, s - 1)
                        wait(pe, kT_lo_made, s + 1 if has(s) else NB)
                        transposed(ps_k, x1[:, j % 2, :]).then_inc(x1T_mm, 1)
                    if g == 1 and has(a):
                        wait(pe, rrep_made, s)
                        project(ps_v[:, 0, :], xT_hi, xT_lo, wqkv_hi, wqkv_lo, 2, is_first).then_inc(v_mm, 1)
                    if g == 2 and has(s - 1):
                        wait(pe, oT_lo_made, s)
                        wait(pe, v_made, s + 2 if has(a) else NB)
                        if isinstance(s, int) and s == 1:
                            wait(pe, w_lo_made, 7)
                        project(ps_v[:, 0, :], oT_hi, oT_lo, wo_hi, wo_lo, 0).then_inc(wo_mm, 1)

            steps(pe, step)


def constants():
    inv_freq = (np.float32(1.0) / np.float32(THETA) ** (np.arange(0, HD, 2, dtype=np.float32) / np.float32(HD))).astype(np.float32)
    freqs = np.arange(S, dtype=np.float32)[:, None] * inv_freq[None, :]
    cos, sin = np.cos(freqs), np.sin(freqs)
    trig = np.stack([np.concatenate([cos, cos], 1), np.concatenate([-sin, sin], 1)], 1).astype(np.float32)
    q, k = np.arange(P)[:, None], np.arange(WB * P)[None, :]
    d = q + (WB - 1) * P - k
    seen = (d >= 0) & (d < WINDOW)
    masks = np.stack([np.where(seen & (k >= first * P), 0.0, NEG) for first in (2, 1, 0)], 1).astype(np.float32)
    return trig, np.eye(P, dtype=np.float32), masks


def ffn_phase(nc, W_router_gate, Ws_gu, Ws_down, We_gu, We_down, ident_in, index_in, x1_dram, factor_dram, x1T, gu_raw, gu_loaded, out):
    TN = 512
    NT = S // TN
    BT = TN // P
    UN = (I_SH + E * I_MOE) // P
    NCH = UN // UNITS
    PER = UNITS * NT
    HRING = 4
    RR = 4
    GR = 32

    with ExitStack() as ctx:
        def sb(name, shape, dt=FP32):
            return ctx.enter_context(nc.sbuf_tensor(name, shape, dt))

        def sem(name):
            return ctx.enter_context(nc.semaphore(name))

        x_hi, x_lo = sb("x_hi", [P, KT, S], FP32R), sb("x_lo", [P, KT, S], FP32R)
        wd_raw = sb("wd_raw", [P, UNITS, H])
        gu_hi, gu_lo = sb("gu_hi", [P, 2, KT, 2 * CW], FP32R), sb("gu_lo", [P, 2, KT, 2 * CW], FP32R)
        wd_hi, wd_lo = sb("wd_hi", [P, UNITS, H], FP32R), sb("wd_lo", [P, UNITS, H], FP32R)
        h_hi, h_lo = sb("h_hi", [P, HRING, TN], FP32R), sb("h_lo", [P, HRING, TN], FP32R)
        work = sb("work", [P, 4, TN])
        factor = sb("factor", [P, RR, TN])
        first_raw = factor[:, :, :].rearrange("p r n -> p (r n)")[:, 0:KT // 2 * 2 * CW].rearrange("p (k n) -> p k n", n=2 * CW)
        r_raw = sb("r_raw", [P, KT, NR])
        r_hi, r_lo = (t[:, HRING - 1, :].rearrange("p (k m) -> p k m", k=KT) for t in (h_hi, h_lo))
        ident2 = sb("ident2", [P, P])
        index8 = sb("index8", [P, E])
        logits = sb("logits", [P, NB, NR])
        top = sb("top", [P, NB, 8])
        top_at = sb("top_at", [P, NB, 8], mybir.dt.uint32)
        top_f = sb("top_f", [P, NB, TOP_K])
        hit = sb("hit", [P, TOP_K, NB, E])
        red = sb("red", [P, 2, NB])
        combine = sb("combine", [P, NB, NR])
        bn6, mv, rstd = sb("bn6_y", [P, 2, 6]), sb("mv_y", [P, 2, 2]), sb("rstd_y", [P, 2, 2])
        half = sb("half_y", [P, 1])
        y = x1T[:, :, :].rearrange("p k s -> p (k s)").rearrange("p (b n) -> p b n", n=H)

        def bank(name):
            return ctx.enter_context(nc.psum_tensor(name, [P, TN], FP32))

        gate_ps = [bank(f"gate_ps{i}") for i in range(2)]
        up_ps = [bank(f"up_ps{i}") for i in range(2)]
        down_ps = [bank(f"down_ps{i}") for i in range(BT)]

        wd_loaded, y_loaded, small_loaded, stored = map(sem, ("wd_loaded", "y_loaded", "small_loaded", "stored"))
        x_hi_made, x_lo_made, r_hi_made, r_lo_made, r_cleared = map(sem, ("x_hi_made", "x_lo_made", "r_hi_made", "r_lo_made", "r_cleared"))
        gu_hi_made, gu_lo_made, wd_hi_made, wd_lo_made = map(sem, ("gu_hi_made", "gu_lo_made", "wd_hi_made", "wd_lo_made"))
        gate_mm, up_mm, down_mm, logitT_mm, logit_mm = map(sem, ("gate_mm", "up_mm", "down_mm", "logitT_mm", "logit_mm"))
        silu_made, up_scaled, h_made, h_hi_made, h_lo_made, y_added = map(sem, ("silu_made", "up_scaled", "h_made", "h_hi_made", "h_lo_made", "y_added"))
        logitT_made, exp_made, route, combine_made = map(sem, ("logitT_made", "router_exp_made", "route", "combine_made"))
        shared_made = sem("shared_made")
        combineT_mm, combineT_made, factors_stored = map(sem, ("combineT_mm", "combineT_made", "factors_stored"))
        factor_loaded = [sem(f"factor_loaded{i}") for i in range(RR)]
        y_bn, y_mv, y_var, y_rstd, y_normed, pool_ready = map(sem, ("y_bn", "y_mv", "y_var", "y_rstd", "y_normed", "pool_ready"))

        def chunks(engine, chunk):
            for c in (0, 1):
                chunk(c, c)
            with engine.Fori(0, (NCH - 3) // 2) as i:
                for k in (2, 3):
                    chunk(2 * i + k, k % 2)
            chunk(NCH - 1, (NCH - 1) % 2)

        def is_chunk(c, n):
            return isinstance(c, int) and c == n

        def raw_gu(c, k):
            return first_raw[:, k - KT // 2, :] if is_chunk(c, 0) and k >= KT // 2 else gu_raw[:, k % 2, :]

        X_PARTS = [(slice(k, k + 1), slice(0, TN)) for k in range(KT)] + [(slice(0, KT), slice(tt * TN, (tt + 1) * TN)) for tt in range(1, NT)]

        block = ctx.enter_context(nc.Block())

        @block.sync
        def _(sp):
            def parts(c):
                return pieces(c, Ws_gu, Ws_down, We_gu, We_down)

            def load_wd(c):
                cuts = {0, P, 2 * P, CW} | {at for at, *_ in parts(c)}
                if len(cuts) == 4:
                    cuts.add(P // 2)
                cuts = sorted(cuts)
                for lo, hi in zip(cuts, cuts[1:]):
                    at, _, _, _, dn, col = [p for p in parts(c) if p[0] <= lo][-1]
                    sp.dma_start(wd_raw[lo % P:lo % P + hi - lo, lo // P, :], dn[col + lo - at:col + hi - at, :]).then_inc(wd_loaded, 16)

            load_gu(sp, first_raw, parts(0), 1, gu_loaded)
            sp.dma_start(r_raw[:, :, :], W_router_gate.rearrange("(k p) n -> p k n", p=P)).then_inc(small_loaded, 16)
            sp.dma_start(ident2[:, :], ident_in).then_inc(small_loaded, 16)
            sp.dma_start(index8[:, :], index_in).then_inc(small_loaded, 16)
            load_wd(0)
            sp.wait_ge(x_lo_made, len(X_PARTS))
            sp.dma_start(y, x1_dram.rearrange("(b p) n -> p b n", p=P)).then_inc(y_loaded, 16)

            for c in range(1, NCH):
                sp.wait_ge(gu_lo_made, KT * c)
                load_gu(sp, gu_raw, parts(c), 0, gu_loaded)
                sp.wait_ge(wd_lo_made, UNITS * c)
                load_wd(c)
                sp.wait_ge(gu_lo_made, KT * c + KT // 2)
                load_gu(sp, gu_raw, parts(c), 1, gu_loaded)
                if c == 1:
                    for tt in range(NT):
                        sp.wait_ge(combineT_made, tt + 1)
                        cols = slice(tt * TN, (tt + 1) * TN)
                        shared = factor[E:E + 1, tt, :].unsqueeze(1).to_broadcast([1, I_SH // GR, TN])
                        routed = factor[0:E, tt, :].unsqueeze(1).to_broadcast([E, I_MOE // GR, TN])
                        sp.dma_start(factor_dram[0:I_SH // GR, cols].unsqueeze(0), shared).then_inc(factors_stored, 16)
                        sp.dma_start(factor_dram[I_SH // GR:, cols].rearrange("(e j) n -> e j n", e=E), routed).then_inc(factors_stored, 16)

            out_v = out.rearrange("(b p) n -> b p n", p=P)
            for b in range(NB):
                wait(sp, y_normed, b + 1)
                sp.dma_start(out_v[b], y[:, b, :]).then_inc(stored, 16)
            sp.wait_ge(stored, 16 * NB)

        @block.gpsimd
        def _(pool):
            pool.memset(r_hi[:, :, :].bitcast(FP32), 0.0).then_inc(r_cleared, 1)
            pool.memset(r_lo[:, :, :].bitcast(FP32), 0.0).then_inc(r_cleared, 1)
            pool.memset(half[:, :], -0.5).then_inc(pool_ready, 1)
            pool.wait_ge(pool_ready, 1)
            for b in range(NB):
                pool.wait_ge(y_mv, b + 1)
                nc.gpsimd.tensor_scalar(rstd[:, b % 2, 1:2], mv[:, b % 2, 1:2], 1.0, LN_EPS, ALU.mult, ALU.add).then_inc(y_var, 1)
                pool.wait_ge(y_var, b + 1)
                nc.gpsimd.tensor_tensor(rstd[:, b % 2, 0:1], rstd[:, b % 2, 1:2], half[:, :], ALU.pow).then_inc(y_rstd, 1)

        @block.scalar
        def _(act):
            def split_x(i):
                ks, cols = X_PARTS[i]
                nc.scalar.copy(x_hi[:, ks, cols], x1T[:, ks, cols]).then_inc(x_hi_made, 1)

            def split_router():
                act.wait_ge(small_loaded, 48)
                act.wait_ge(r_cleared, 2)
                nc.scalar.copy(r_hi[:, :, 0:NR], r_raw[:, :, :]).then_inc(r_hi_made, 1)

            def split_gu(c, par, ks):
                for k in ks:
                    wait(act, gu_loaded, 16 * GU_LOADS * (2 * c + k // 2 + 1))
                    nc.scalar.copy(gu_hi[:, par, k, :], raw_gu(c, k)).then_inc(gu_hi_made, 1)

            def split_wd(c):
                wait(act, wd_loaded, 64 * (c + 1))
                wait(act, down_mm, BT * NT * c)
                for u in range(UNITS):
                    nc.scalar.copy(wd_hi[:, u, :], wd_raw[:, u, :]).then_inc(wd_hi_made, 1)

            def load_factor(c, m):
                cc, m = (c, m) if m < PER else (c + 1, m - PER)
                if isinstance(cc, int) and not 0 < cc < NCH:
                    return
                tt, u = divmod(m, UNITS)
                if is_chunk(cc, 1) and m == 0:
                    act.wait_ge(factors_stored, 32 * NT)
                if not (is_chunk(cc, 1) and m < RR):
                    wait(act, up_scaled, PER * (cc - 1) + m - RR + 1)
                first_row = P // GR * (UNITS * cc + u)
                src = factor_dram[bass.ds(first_row, P // GR), tt * TN:(tt + 1) * TN]
                act.dma_start(factor[:, m % RR, :], src.unsqueeze(1).to_broadcast([P // GR, GR, TN])).then_inc(factor_loaded[m % RR], 16)

            def router(tt):
                if tt == 0:
                    split_router()
                    act.wait_ge(gu_lo_made, KT)
                    for i in range(NT):
                        act.wait_ge(logitT_mm, i + 1)
                        nc.scalar.copy(factor[0:NR, i, :], down_ps[i][0:NR, :]).then_inc(logitT_made, 1)
                if tt == 2:
                    for i in range(NT):
                        act.wait_ge(combineT_mm, i + 1)
                        nc.scalar.copy(factor[0:NR, i, :], down_ps[i][0:NR, :]).then_inc(combineT_made, 1)

            for k in range(KT):
                split_gu(0, 0, [k])
                split_x(k)
            split_x(KT)

            def chunk(c, par):
                for tt in range(NT):
                    for u in range(UNITS):
                        m = UNITS * tt + u
                        n = PER * c + m
                        wait(act, gate_mm, n + 1)
                        wait(act, h_made, n - 1)
                        nc.scalar.activation(work[:, m % 2, :], gate_ps[m % 2][:, :], ACT.Silu).then_inc(silu_made, 1)
                        load_factor(c, m + RR - 1)
                        wait(act, h_made, n + 1)
                        wait(act, down_mm, BT * (NT * c + tt + (u - HRING) // UNITS + 1))
                        nc.scalar.copy(h_hi[:, m % HRING, :], work[:, 2 + m % 2, :]).then_inc(h_hi_made, 1)
                        if is_chunk(c, 0) and tt == 0 and u < 2:
                            split_x(KT + 1 + u)
                        if tt == 0 and u == 1:
                            split_wd(c)
                        if tt >= 1 and u == 1 and not is_chunk(c, NCH - 1):
                            split_gu(c + 1, 1 - par, {1: (0, 1), 2: (2,), 3: (3,)}[tt])
                        if is_chunk(c, 0) and tt == 1 and u == 0:
                            act.wait_ge(route, 3)
                            nc.scalar.activation(logits[:, :, :], logits[:, :, :], ACT.Exp).then_inc(exp_made, 1)
                    if is_chunk(c, 0):
                        router(tt)

            chunks(act, chunk)

        @block.vector
        def _(dve):
            def split_x(i):
                ks, cols = X_PARTS[i]
                dve.wait_ge(x_hi_made, i + 1)
                nc.vector.tensor_tensor(x_lo[:, ks, cols], x1T[:, ks, cols], x_hi[:, ks, cols].bitcast(FP32), ALU.subtract).then_inc(x_lo_made, 1)

            def split_router():
                dve.wait_ge(r_hi_made, 1)
                nc.vector.tensor_tensor(r_lo[:, :, 0:NR], r_raw[:, :, :], r_hi[:, :, 0:NR].bitcast(FP32), ALU.subtract).then_inc(r_lo_made, 1)

            def split_gu(c, par, ks):
                for k in ks:
                    wait(dve, gu_hi_made, KT * c + k + 1)
                    nc.vector.tensor_tensor(gu_lo[:, par, k, :], raw_gu(c, k), gu_hi[:, par, k, :].bitcast(FP32), ALU.subtract).then_inc(gu_lo_made, 1)

            def split_wd(c):
                for u in range(UNITS):
                    wait(dve, wd_hi_made, UNITS * c + u + 1)
                    nc.vector.tensor_tensor(wd_lo[:, u, :], wd_raw[:, u, :], wd_hi[:, u, :].bitcast(FP32), ALU.subtract).then_inc(wd_lo_made, 1)

            steps_done = [0]

            def link(instruction):
                steps_done[0] += 1
                instruction.then_inc(route, 1)
                dve.wait_ge(route, steps_done[0])

            def router_logits():
                dve.wait_ge(logit_mm, 1)
                link(nc.vector.tensor_copy(logits[:, :, :], down_ps[0][:, 0:NB * 16].rearrange("p (b n) -> p b n", n=16)[:, :, 0:NR]))
                link(nc.vector.tensor_reduce(red[:, 0, :], logits[:, :, 0:E], mybir.AxisListType.X, ALU.max))
                nc.vector.tensor_scalar(logits[:, :, E], logits[:, :, E], -1.0, None, ALU.mult)
                link(nc.vector.tensor_tensor(logits[:, :, 0:E], logits[:, :, 0:E], red[:, 0, :].unsqueeze(2).to_broadcast([P, NB, E]), ALU.subtract))

            def router_probs():
                dve.wait_ge(exp_made, 1)
                link(nc.vector.tensor_reduce(red[:, 0, :], logits[:, :, 0:E], mybir.AxisListType.X, ALU.add))
                link(nc.vector.reciprocal(red[:, 1, :], red[:, 0, :]))
                link(nc.vector.tensor_tensor(logits[:, :, 0:E], logits[:, :, 0:E], red[:, 1, :].unsqueeze(2).to_broadcast([P, NB, E]), ALU.mult))
                link(nc.vector.tensor_scalar(red[:, 0, :], logits[:, :, E], 1.0, None, ALU.add))
                nc.vector.reciprocal(combine[:, :, E], red[:, 0, :]).then_inc(shared_made, 1)
                for b in range(NB):
                    last = nc.vector.max(top[:, b, :], logits[:, b, 0:E])
                link(last)

            def router_top():
                for b in range(NB):
                    last = nc.vector.max_index(top_at[:, b, :], top[:, b, :], logits[:, b, 0:E])
                link(last)
                link(nc.vector.tensor_copy(top_f[:, :, :], top_at[:, :, 0:TOP_K]))
                for t in range(TOP_K):
                    last = nc.vector.tensor_tensor(hit[:, t, :, :], top_f[:, :, t:t + 1].to_broadcast([P, NB, E]),
                                                   index8[:, :].unsqueeze(1).to_broadcast([P, NB, E]), ALU.is_equal)
                link(last)
                link(nc.vector.tensor_tensor(hit[:, 0, :, :], hit[:, 0, :, :], hit[:, 1, :, :], ALU.add))
                nc.vector.tensor_tensor(combine[:, :, 0:E], logits[:, :, 0:E], hit[:, 0, :, :], ALU.mult).then_inc(combine_made, 1)

            for k in range(KT):
                split_gu(0, 0, [k])
                split_x(k)
            split_x(KT)

            def add_down(c, tt):
                turn = NT * c + tt
                for i in range(BT):
                    b = BT * tt + i
                    wait(dve, down_mm, BT * turn + i + 1)
                    if i == 0:
                        wait(dve, y_added, BT * (turn - NT + 1))
                        if is_chunk(c, 0) and tt == 0:
                            dve.wait_ge(y_loaded, 16)
                            dve.wait_ge(shared_made, 1)
                    if is_chunk(c, 0):
                        nc.vector.scalar_tensor_tensor(y[:, b, :], down_ps[i][:, :], combine[:, b, E:E + 1], y[:, b, :], ALU.mult, ALU.add).then_inc(y_added, 1)
                    else:
                        nc.vector.tensor_tensor(y[:, b, :], down_ps[i][:, :], y[:, b, :], ALU.add).then_inc(y_added, 1)

            def normalise(b):
                dve.wait_ge(y_added, BT * NT * (NCH - 1) + b + 1)
                nc.vector.bn_stats(bn6[:, b % 2, :], y[:, b, :]).then_inc(y_bn, 1)
                dve.wait_ge(y_bn, b + 1)
                nc.vector.bn_aggr(mv[:, b % 2, :], bn6[:, b % 2, :]).then_inc(y_mv, 1)

            def finish(b):
                dve.wait_ge(y_mv, b + 1)
                dve.wait_ge(y_rstd, b + 1)
                nc.vector.tensor_scalar(y[:, b, :], y[:, b, :], mv[:, b % 2, 0:1], rstd[:, b % 2, 0:1], ALU.subtract, ALU.mult).then_inc(y_normed, 1)

            def chunk(c, par):
                for tt in range(NT):
                    for u in range(UNITS):
                        m = UNITS * tt + u
                        n = PER * c + m
                        h = work[:, 2 + m % 2, :]
                        wait(dve, up_mm, n + 1)
                        wait(dve, h_lo_made, n - 1)
                        if is_chunk(c, 0):
                            wait(dve, silu_made, n + 1)
                            nc.vector.tensor_tensor(h, work[:, m % 2, :], up_ps[m % 2][:, :], ALU.mult).then_inc(h_made, 1)
                        else:
                            wait(dve, factor_loaded[m % RR], 16 * (PER // RR * (c - 1) + m // RR + 1))
                            nc.vector.tensor_tensor(h, up_ps[m % 2][:, :], factor[:, m % RR, :], ALU.mult).then_inc(up_scaled, 1)
                            wait(dve, silu_made, n + 1)
                            wait(dve, up_scaled, n - PER + 1)
                            nc.vector.tensor_tensor(h, work[:, m % 2, :], h, ALU.mult).then_inc(h_made, 1)
                        wait(dve, h_hi_made, n + 1)
                        nc.vector.tensor_tensor(h_lo[:, m % HRING, :], h, h_hi[:, m % HRING, :].bitcast(FP32), ALU.subtract).then_inc(h_lo_made, 1)
                        if is_chunk(c, 0) and tt == 0 and u < 2:
                            split_x(KT + 1 + u)
                        if is_chunk(c, 0) and tt == 1:
                            (router_logits, router_probs, lambda: add_down(0, 0))[u]()
                        elif u == 0 and tt:
                            add_down(c, tt - 1)
                            if is_chunk(c, 0) and tt == 2:
                                router_top()
                            if is_chunk(c, NCH - 1):
                                for b in range(BT * (tt - 1), BT * tt):
                                    normalise(b)
                                    if b % 2:
                                        finish(b - 1)
                                        finish(b)
                        elif u == 0 and not is_chunk(c, 0):
                            add_down(c - 1, NT - 1)
                        if u == 1 and tt == 0:
                            split_wd(c)
                        if tt >= 1 and u == 1 and not is_chunk(c, NCH - 1):
                            split_gu(c + 1, 1 - par, {1: (0, 1), 2: (2,), 3: (3,)}[tt])
                    if tt == 0 and is_chunk(c, 0):
                        split_router()

            chunks(dve, chunk)
            for i in range(BT):
                b = BT * (NT - 1) + i
                turn = NT * NCH - 1
                dve.wait_ge(down_mm, BT * turn + i + 1)
                nc.vector.tensor_tensor(y[:, b, :], down_ps[i][:, :], y[:, b, :], ALU.add).then_inc(y_added, 1)
                normalise(b)
                if i:
                    finish(b - 1)
            finish(NB - 1)

        @block.tensor
        def _(pe):
            def router():
                pe.wait_ge(r_lo_made, 1)
                for tt in range(NT):
                    pe.wait_ge(x_lo_made, KT + tt)
                    cols = slice(tt * TN, (tt + 1) * TN)
                    for k in range(KT):
                        nc.tensor.matmul(down_ps[tt][:, :], r_lo[:, k, :], x_hi[:, k, cols], start=(k == 0), stop=False)
                        nc.tensor.matmul(down_ps[tt][:, :], r_hi[:, k, :], x_lo[:, k, cols], start=False, stop=False)
                        last = nc.tensor.matmul(down_ps[tt][:, :], r_hi[:, k, :], x_hi[:, k, cols], start=False, stop=(k == KT - 1))
                    last.then_inc(logitT_mm, 1)

            def router_rows():
                pe.wait_ge(small_loaded, 48)
                for b in range(NB):
                    pe.wait_ge(logitT_made, b // BT + 1)
                    last = nc.tensor.transpose(down_ps[0][:, 16 * b:16 * b + NR], factor[0:NR, b // BT, (b % BT) * P:(b % BT + 1) * P], ident2[0:NR, 0:NR])
                last.then_inc(logit_mm, 1)

            def gate_up(c, par, tt, u):
                m = UNITS * tt + u
                cols = slice(tt * TN, (tt + 1) * TN)
                wait(pe, h_made, PER * c + m - 1)
                for ps, base, done in ((gate_ps, 0, gate_mm), (up_ps, CW, up_mm)):
                    o = ps[m % 2][:, :]
                    part = slice(base + u * P, base + (u + 1) * P)
                    for k in range(KT):
                        if m == 0 and base == 0:
                            wait(pe, gu_lo_made, KT * c + k + 1)
                        if is_chunk(c, 0) and u == 0 and base == 0:
                            pe.wait_ge(x_lo_made, KT + tt if tt else k + 1)
                        nc.tensor.matmul(o, gu_lo[:, par, k, part], x_hi[:, k, cols], start=(k == 0), stop=False)
                        nc.tensor.matmul(o, gu_hi[:, par, k, part], x_lo[:, k, cols], start=False, stop=False)
                        last = nc.tensor.matmul(o, gu_hi[:, par, k, part], x_hi[:, k, cols], start=False, stop=(k == KT - 1))
                    last.then_inc(done, 1)

            def down(c, tt):
                turn = NT * c + tt
                wait(pe, h_lo_made, UNITS * (turn + 1))
                if tt == 0:
                    wait(pe, wd_lo_made, UNITS * (c + 1))
                if is_chunk(c, 0) and tt == 0:
                    pe.wait_ge(route, 1)
                if is_chunk(c, 0) and tt == 2:
                    pe.wait_ge(combineT_made, NT)
                for i in range(BT):
                    wait(pe, y_added, BT * (turn - 1) + i + 1)
                    tok = slice(i * P, (i + 1) * P)
                    for u in range(UNITS):
                        slot = (UNITS * tt + u) % HRING
                        hh, hl = h_hi[:, slot, tok], h_lo[:, slot, tok]
                        nc.tensor.matmul(down_ps[i][:, :], hl, wd_hi[:, u, :], start=(u == 0), stop=False)
                        nc.tensor.matmul(down_ps[i][:, :], hh, wd_lo[:, u, :], start=False, stop=False)
                        last = nc.tensor.matmul(down_ps[i][:, :], hh, wd_hi[:, u, :], start=False, stop=(u == UNITS - 1))
                    last.then_inc(down_mm, 1)

            def chunk(c, par):
                for tt in range(NT):
                    for u in range(UNITS):
                        gate_up(c, par, tt, u)
                        if is_chunk(c, 0) and tt == 1 and u == 0:
                            router_rows()
                        if u == 0 and tt:
                            down(c, tt - 1)
                        elif u == 0 and not is_chunk(c, 0):
                            down(c - 1, NT - 1)
                    if tt == 0 and is_chunk(c, 0):
                        router()
                    if tt == 2 and is_chunk(c, 0):
                        pe.wait_ge(combine_made, 1)
                        for i in range(NT):
                            pe.wait_ge(y_added, BT + i + 1)
                            for b in range(BT * i, BT * (i + 1)):
                                last = nc.tensor.transpose(down_ps[i][0:NR, (b % BT) * P:(b % BT + 1) * P], combine[:, b, :], ident2[:, :])
                            last.then_inc(combineT_mm, 1)

            chunks(pe, chunk)
            down(NCH - 1, NT - 1)




def kernel(L0_attn_hidden_states, L0_attn_Wqkv, L0_attn_q_norm_w, L0_attn_k_norm_w, L0_attn_Wo,
           L0_ffn_W_router, L0_ffn_W_sgate, L0_ffn_Ws_gate_up, L0_ffn_Ws_down, L0_ffn_We_gate_up, L0_ffn_We_down):
    import concourse.bacc as bacc
    from concourse.bass_utils import run_bass_kernel_spmd

    trig, ident, masks = constants()
    nc = bacc.Bacc("TRN2", target_bir_lowering=False, num_devices=1)
    arrays = {
        "x": np.asarray(L0_attn_hidden_states).reshape(S, H),
        "Wqkv": L0_attn_Wqkv, "q_w": L0_attn_q_norm_w, "k_w": L0_attn_k_norm_w, "Wo": L0_attn_Wo,
        "W_router_gate": np.concatenate([np.asarray(L0_ffn_W_router), np.asarray(L0_ffn_W_sgate)], 0).T,
        "Ws_gu": L0_ffn_Ws_gate_up, "Ws_down": L0_ffn_Ws_down, "We_gu": L0_ffn_We_gate_up, "We_down": L0_ffn_We_down,
        "trig": trig, "ident_c": ident, "masks_c": masks,
        "index_c": np.tile(np.arange(E, dtype=np.float32), (P, 1)),
    }
    arrays = {f"in_{n}": np.ascontiguousarray(a) for n, a in arrays.items()}
    a = {n[3:]: nc.dram_tensor(n, v.shape, mybir.dt.from_np(v.dtype), kind="ExternalInput").ap() for n, v in arrays.items()}
    out = nc.dram_tensor("out_dram", (S, H), FP32, kind="ExternalOutput").ap()
    x1_dram = nc.dram_tensor("x1_dram", (S, H), FP32, kind="Internal").ap()
    factor_dram = nc.dram_tensor("factor_dram", ((I_SH + E * I_MOE) // 32, S), FP32, kind="Internal").ap()
    with nc.sbuf_tensor("x1T", [P, KT, S], FP32) as x1T, nc.sbuf_tensor("gu_raw", [P, KT // 2, 2 * CW], FP32) as gu_raw, \
            nc.semaphore("gu_loaded") as gu_loaded:

        def load_ahead(sp):
            load_gu(sp, gu_raw, pieces(0, a["Ws_gu"], a["Ws_down"], a["We_gu"], a["We_down"]), 0, gu_loaded)

        attention_phase(nc, a["x"], a["Wqkv"], a["q_w"], a["k_w"], a["Wo"], a["trig"], a["ident_c"], a["masks_c"], x1_dram, x1T, load_ahead)
        ffn_phase(nc, a["W_router_gate"], a["Ws_gu"], a["Ws_down"], a["We_gu"], a["We_down"], a["ident_c"], a["index_c"],
                  x1_dram, factor_dram, x1T, gu_raw, gu_loaded, out)
    r = run_bass_kernel_spmd(nc, [arrays], core_ids=[0])
    return r.results[0]["out_dram"].reshape(1, S, H)
```

```python
import numpy as np
import concourse.bass as bass
from concourse import mybir
from contextlib import ExitStack

FP32 = mybir.dt.float32
FP32R = mybir.dt.float32r
ALU = mybir.AluOpType
ACT = mybir.ActivationFunctionType

P = 128
S = 2048
H = 512
NH, HD = 16, 32
KT = H // P
NB = S // P
WINDOW = 256
WB = WINDOW // P + 1
RING = 4
GROUPS = NH // 4
SCALE = 1.0 / HD ** 0.5
RMS_EPS, LN_EPS = 1e-6, 1e-5
NEG = -1e30
THETA = 10000.0

E, TOP_K, I_MOE, I_SH = 8, 2, 352, 1408
NR = E + 1


def wait(engine, semaphore, value):
    if isinstance(value, int) and value <= 0:
        return
    engine.wait_ge(semaphore, value)


def wait_apart(engine, semaphore, value, passed):
    wait(engine, semaphore, value)
    if not isinstance(value, int):
        engine.sem_inc(passed, 1)


UNITS = 3
CW = UNITS * P
GU_LOADS = 4


def pieces(c, Ws_gu, Ws_down, We_gu, We_down):
    found = []
    at, end = c * CW, (c + 1) * CW
    while at < end:
        if at < I_SH:
            gu, dn, n_in, col = Ws_gu, Ws_down, I_SH, at
        else:
            e, col = divmod(at - I_SH, I_MOE)
            gu, dn, n_in = We_gu[e], We_down[e], I_MOE
        n = min(end - at, n_in - col)
        if n == CW:
            n = CW - P
        found.append((at - c * CW, n, gu, n_in, dn, col))
        at += n
    return found


def load_gu(sp, dst, parts, half, loaded):
    rows = slice(half * H // 2, (half + 1) * H // 2)
    for at, n, gu, up, _, col in parts:
        for base, src in ((0, col), (CW, up + col)):
            sp.dma_start(dst[:, :, base + at:base + at + n],
                         gu[rows, src:src + n].rearrange("(k p) n -> p k n", p=P)).then_inc(loaded, 16)


KEY_SLOTS = RING + WB - 1


def window(j):
    return (j - WB + 1) % RING


def key_slot(j):
    return window(j) + WB - 1


def attention_phase(nc, x, xT, Wqkv, q_w, k_w, Wo, trig, ident_in, masks_in, x1_dram, x1T, load_ahead):
    with ExitStack() as ctx:
        def sb(name, shape, dt=FP32):
            return ctx.enter_context(nc.sbuf_tensor(name, shape, dt))

        def sem(name):
            return ctx.enter_context(nc.semaphore(name))

        ident = sb("ident", [P, P])
        mask = sb("mask", [P, WB * P])
        qw_b, kw_b = sb("qw_b", [P, H]), sb("kw_b", [P, H])
        wqkv_hi, wqkv_lo = sb("wqkv_hi", [P, KT, 3 * H], FP32R), sb("wqkv_lo", [P, KT, 3 * H], FP32R)
        wo_hi, wo_lo = sb("wo_hi", [P, KT, H], FP32R), sb("wo_lo", [P, KT, H], FP32R)
        half = sb("half", [P, 1])
        x_in, xT_in = sb("x_in", [P, H]), sb("xT_in", [P, KT, P])
        cs = sb("cs", [P, 2, 2, HD])
        xT_hi, xT_lo = sb("xT_hi", [P, 2, KT, P], FP32R), sb("xT_lo", [P, 2, KT, P], FP32R)
        qk = sb("qk", [P, 2, H])
        rot_a, rot_b = sb("rot_a", [P, H]), sb("rot_b", [P, H])
        scratch = sb("scratch", [P, H])
        ssq, rms = sb("ssq", [P, 2]), sb("rms", [P, 4])
        qT_hi, qT_lo = sb("qT_hi", [P, 2, KT, P], FP32R), sb("qT_lo", [P, 2, KT, P], FP32R)
        kT_hi, kT_lo = sb("kT_hi", [P, KT, KEY_SLOTS, P], FP32R), sb("kT_lo", [P, KT, KEY_SLOTS, P], FP32R)
        v_ring = sb("v_ring", [P, RING, H])
        prob = sb("prob", [P, 2, 4, WB * P])
        probT = sb("probT", [P, 2, 4, WB * P])
        nbias, rsum = sb("nbias", [P, 2, NH]), sb("rsum", [P, 2, NH])
        rinv = sb("rinv", [P, NH])
        oT = sb("oT", [P, H])
        oT_hi, oT_lo = sb("oT_hi", [P, KT, P], FP32R), sb("oT_lo", [P, KT, P], FP32R)
        res = sb("res", [P, H])
        bn6, mv, rstd = sb("bn6", [P, 6]), sb("mv", [P, 2]), sb("rstd", [P, 2])
        x1 = sb("x1", [P, 2, H])
        early_masks = x1[:, :, 0:WB * P]

        def bank(name, n=1):
            return ctx.enter_context(nc.psum_tensor(name, [P, n, H], FP32))

        score_ps = [bank(f"score_ps{i}") for i in range(2)]
        probT_ps = bank("probT_ps", 2)
        oT_ps = bank("oT_ps")
        ps_q, ps_k, ps_v = bank("ps_q"), bank("ps_k"), bank("ps_v")

        w_loaded = [sem(f"w_loaded_{part}") for part in ("q", "k", "v", "o", "q_second")]
        ident_loaded, const_loaded = sem("ident_loaded"), sem("const_loaded")
        x_loaded, xT_loaded, cs_loaded = sem("x_loaded"), sem("xT_loaded"), [sem(f"cs_loaded{i}") for i in range(2)]
        x1_stored = sem("x1_stored")
        passed = {e: sem(f"{e}_waits_passed") for e in ("dve", "pool", "sp")}
        w_hi_made, w_lo_made, cleared = sem("w_hi_made"), sem("w_lo_made"), sem("cleared")
        q_mm, k_mm, v_mm, qT_mm, kT_mm = map(sem, ("q_mm", "k_mm", "v_mm", "qT_mm", "kT_mm"))
        score_mm, probT_mm, pv_mm = map(sem, ("score_mm", "probT_mm", "pv_mm"))
        rrep_mm, wo_mm, x1T_mm = map(sem, ("rrep_mm", "wo_mm", "x1T_mm"))
        xT_hi_made, q_sq, k_sq, v_made, exp_made = map(sem, ("xT_hi_made", "q_sq", "k_sq", "v_made", "exp_made"))
        probT_act, rrep_made, oT_hi_made = map(sem, ("probT_act", "rrep_made", "oT_hi_made"))
        x1T_made, qT_hi_made, kT_hi_made = map(sem, ("x1T_made", "qT_hi_made", "kT_hi_made"))
        xT_lo_made, q_normed, k_normed, masked = map(sem, ("xT_lo_made", "q_normed", "k_normed", "masked"))
        probT_dve, rinv_made, rinv_spread, oT_made, oT_lo_made = map(sem, ("probT_dve", "rinv_made", "rinv_spread", "oT_made", "oT_lo_made"))
        res_made, bn_made, mv_made, x1_made = map(sem, ("res_made", "bn_made", "mv_made", "x1_made"))
        qT_lo_made, kT_lo_made = map(sem, ("qT_lo_made", "kT_lo_made"))
        q_var, k_var, q_rms, k_rms = map(sem, ("q_var", "k_var", "q_rms", "k_rms"))
        q_part, k_part, q_rot, k_rot = map(sem, ("q_part", "k_part", "q_rot", "k_rot"))
        ln_var, ln_rstd, kT_copied = map(sem, ("ln_var", "ln_rstd", "kT_copied"))

        staged = x1T[:, :, :].rearrange("p k s -> p (k s)")
        wqkv_raw = staged[:, 0:KT * 3 * H].rearrange("p (k n) -> p k n", k=KT)
        wo_raw = staged[:, KT * 3 * H:].rearrange("p (k n) -> p k n", k=KT)

        def steps(engine, step):
            for s in (-1, 0, 1):
                step(s, s % RING, s // RING)
            with engine.Fori(0, 3) as i:
                for j in range(RING):
                    s0 = 2 + j
                    step(RING * i + s0, s0 % RING, i + s0 // RING)
            for s in range(14, 18):
                step(s, s % RING, s // RING)

        def v_group(s):
            return 1 if isinstance(s, int) and s == -1 else 3

        def has(block):
            return not isinstance(block, int) or 0 <= block < NB

        def rotate(queue, engine, n, slot, turn, c, temp_a, temp_b, normed, part, rotated):
            heads = qk[:, c, :].rearrange("p (h d) -> p h d", d=HD)
            a = temp_a.rearrange("p (h d) -> p h d", d=HD)
            b = temp_b.rearrange("p (h d) -> p h d", d=HD)
            cos = cs[:, slot, 0:1, :].to_broadcast([P, NH, HD])
            sin = cs[:, slot, 1:2, :]
            wait(queue, cs_loaded[slot], 16 * (turn + 1))
            wait(queue, normed, n + 1)
            engine.tensor_tensor(a, heads, cos, ALU.mult).then_inc(part, 1)
            lo, hi = slice(0, HD // 2), slice(HD // 2, HD)
            engine.tensor_tensor(b[:, :, lo], heads[:, :, hi], sin[:, :, lo].to_broadcast([P, NH, HD // 2]), ALU.mult).then_inc(part, 1)
            engine.tensor_tensor(b[:, :, hi], heads[:, :, lo], sin[:, :, hi].to_broadcast([P, NH, HD // 2]), ALU.mult).then_inc(part, 1)
            wait(queue, part, 3 * (n + 1))
            engine.tensor_tensor(heads, a, b, ALU.add).then_inc(rotated, 1)

        block = ctx.enter_context(nc.Block())

        @block.sync
        def _(sp):
            def load_xT(n, slot):
                sp.dma_start(xT_in[:, :, :], xT.rearrange("(k p) t -> p k t", p=P)[:, :, bass.ts(n, P)]).then_inc(xT_loaded, 16)
                sp.dma_start(cs[:, slot, :, :], trig[bass.ts(n, P), :, :]).then_inc(cs_loaded[slot], 16)

            sp.dma_start(ident[:, :], ident_in).then_inc(ident_loaded, 16)
            load_xT(0, 0)
            for i, loaded in ((0, w_loaded[0]), (1, w_loaded[4])):
                sp.dma_start(wqkv_raw[:, 2 * i:2 * i + 2, 0:H], Wqkv[i * H // 2:(i + 1) * H // 2, 0:H].rearrange("(k p) n -> p k n", p=P)).then_inc(loaded, 16)
            for c in range(1, 3):
                sp.dma_start(wqkv_raw[:, :, c * H:(c + 1) * H], Wqkv[:, c * H:(c + 1) * H].rearrange("(k p) n -> p k n", p=P)).then_inc(w_loaded[c], 16)
            sp.dma_start(qw_b[:, :], q_w.partition_broadcast(P)).then_inc(const_loaded, 16)
            sp.dma_start(kw_b[:, :], k_w.partition_broadcast(P)).then_inc(const_loaded, 16)
            sp.dma_start(early_masks, masks_in[:, 0:2, :]).then_inc(const_loaded, 16)
            sp.dma_start(mask[:, :], masks_in[:, 2, :]).then_inc(const_loaded, 16)
            sp.dma_start(wo_raw, Wo.rearrange("(k p) n -> p k n", p=P)).then_inc(w_loaded[3], 16)
            sp.wait_ge(xT_lo_made, 1)
            load_xT(1, 1)

            def step(s, j, turn):
                if isinstance(s, int) and s < 0:
                    return
                if isinstance(s, int) and s == 1:
                    load_ahead(sp)
                if has(s + 2):
                    wait_apart(sp, xT_lo_made, s + 2, passed["sp"])
                    wait(sp, q_rot, s + 1)
                    wait(sp, k_rot, s + 1)
                    load_xT(s + 2, j % 2)
                if has(s - 1):
                    wait_apart(sp, res_made, s - 1, passed["sp"])
                    sp.dma_start(x_in[:, :], x[bass.ts(s - 1, P), :]).then_inc(x_loaded, 16)
                if has(s - 2):
                    wait(sp, x1_made, s - 1)
                    sp.dma_start(x1_dram[bass.ts(s - 2, P), :], x1[:, j % 2, :]).then_inc(x1_stored, 16)
                    wait_apart(sp, x1_stored, 16 * (s - 1), passed["sp"])

            steps(sp, step)

        @block.gpsimd
        def _(pool):
            pool.memset(half[:, :], -0.5).then_inc(cleared, 1)
            pool.memset(v_ring[:, 2:4, :], 0.0).then_inc(cleared, 1)
            pool.memset(kT_hi[:, :, 2:4, :].bitcast(FP32), 0.0).then_inc(cleared, 1)
            pool.memset(kT_lo[:, :, 2:4, :].bitcast(FP32), 0.0).then_inc(cleared, 1)
            pool.wait_ge(cleared, 4)

            def rms_of(n, c, squares, var, rms_ready):
                wait_apart(pool, squares, n + 1, passed["pool"])
                nc.gpsimd.tensor_scalar(rms[:, 2 + c:3 + c], ssq[:, c:c + 1], 1.0 / H, RMS_EPS, ALU.mult, ALU.add).then_inc(var, 1)
                wait(pool, var, n + 1)
                nc.gpsimd.tensor_tensor(rms[:, c:c + 1], rms[:, 2 + c:3 + c], half[:, :], ALU.pow).then_inc(rms_ready, 1)


            def step(s, j, turn):
                a, slot = s + 1, (j + 1) % RING
                a_slot, a_turn = (j + 1) % 2, 2 * turn + (j + 1) // 2
                if has(a):
                    rms_of(a, 0, q_sq, q_var, q_rms)
                    if not (isinstance(a, int) and a == 0):
                        wait(pool, q_rot, a)
                        wait(pool, k_rot, a)
                    if isinstance(a, int) and a == 0:
                        rms_of(a, 1, k_sq, k_var, k_rms)
                    else:
                        rotate(pool, nc.gpsimd, a, a_slot, a_turn, 0, rot_a[:, :], rot_b[:, :], q_normed, q_part, q_rot)
                        rms_of(a, 1, k_sq, k_var, k_rms)
                        wait(pool, q_rot, a + 1)
                        rotate(pool, nc.gpsimd, a, a_slot, a_turn, 1, rot_a[:, :], rot_b[:, :], k_normed, k_part, k_rot)
                if has(s - 1):
                    wait_apart(pool, mv_made, s, passed["pool"])
                    nc.gpsimd.tensor_scalar(rstd[:, 1:2], mv[:, 1:2], 1.0, LN_EPS, ALU.mult, ALU.add).then_inc(ln_var, 1)
                    wait(pool, ln_var, s)
                    nc.gpsimd.tensor_tensor(rstd[:, 0:1], rstd[:, 1:2], half[:, :], ALU.pow).then_inc(ln_rstd, 1)
                if has(a) and key_slot(slot) != slot:
                    wait_apart(pool, kT_lo_made, a + 1, passed["pool"])
                    for keys in (kT_hi, kT_lo):
                        nc.gpsimd.tensor_copy(keys[:, :, slot, :], keys[:, :, key_slot(slot), :]).then_inc(kT_copied, 1)

            steps(pool, step)

        @block.scalar
        def _(act):
            def split_wqkv(c):
                act.wait_ge(w_loaded[c], 16)
                for i in range(2):
                    if c == 0 and i == 1:
                        act.wait_ge(w_loaded[4], 16)
                    part = (slice(None), slice(2 * i, 2 * i + 2), slice(c * H, (c + 1) * H))
                    nc.scalar.copy(wqkv_hi[part], wqkv_raw[part]).then_inc(w_hi_made, 1)

            def split_wo(k):
                act.wait_ge(w_loaded[3], 16)
                nc.scalar.copy(wo_hi[:, k, :], wo_raw[:, k, :]).then_inc(w_hi_made, 1)

            def exps(s, j, g, pair):
                for h in (2 * pair, 2 * pair + 1):
                    head = 4 * g + h
                    wait(act, masked, NH * s + head + 1)
                    p = prob[:, g % 2, h, :]
                    nc.scalar.activation(p, p, ACT.Exp, bias=nbias[:, j % 2, head:head + 1], scale=-1.0,
                                         accum_out=rsum[:, j % 2, head:head + 1]).then_inc(exp_made, 1)

            def probT_out(G, half):
                wait(act, probT_mm, 2 * G + 2)
                nc.scalar.copy(probT[:, half, 2:4, :], probT_ps[:, :, 0:WB * P]).then_inc(probT_act, 1)

            def split_xT(b, slot):
                wait(act, xT_loaded, 16 * (b + 1))
                wait(act, v_mm, b - 1)
                nc.scalar.copy(xT_hi[:, slot, :, :], xT_in[:, :, :]).then_inc(xT_hi_made, 1)

            split_xT(0, 0)
            split_wqkv(0)
            split_wqkv(1)

            def step(s, j, turn):
                a = s + 1
                for g in range(GROUPS):
                    if g == 2 and has(s + 2):
                        split_xT(s + 2, j % 2)
                    if g == 1 and has(s - 2):
                        wait(act, x1T_mm, s - 1)
                        nc.scalar.copy(x1T[:, :, bass.ts(s - 2, P)], ps_k[:, 0, :].rearrange("p (k t) -> p k t", k=KT)).then_inc(x1T_made, 1)
                    if isinstance(s, int) and s == 0:
                        split_wo(g)
                    if has(s):
                        exps(s, j, g, 0)
                    if g == 3 and has(a):
                        wait(act, qT_mm, a + 1)
                        nc.scalar.copy(qT_hi[:, (j + 1) % 2, :, :], ps_q[:, 0, :].rearrange("p (k t) -> p k t", k=KT)).then_inc(qT_hi_made, 1)
                    if has(s) if g else has(s - 1):
                        probT_out(4 * s + g - 1, (g - 1) % 2)
                    if g == 3 and has(a):
                        wait(act, kT_mm, a + 1)
                        nc.scalar.copy(kT_hi[:, :, key_slot(j + 1), :], ps_k[:, 0, :].rearrange("p (k t) -> p k t", k=KT)).then_inc(kT_hi_made, 1)
                    if g == 0 and has(a):
                        wait(act, q_mm, a + 1)
                        if has(s - 1):
                            wait(act, rrep_mm, s)
                        nc.scalar.activation(scratch[:, :], ps_q[:, 0, :], ACT.Square, accum_out=ssq[:, 0:1]).then_inc(q_sq, 1)
                        if isinstance(s, int) and s == -1:
                            split_wqkv(2)
                    if g == 1 and has(a):
                        wait(act, k_mm, a + 1)
                        wait(act, q_sq, a + 1)
                        nc.scalar.activation(scratch[:, :], ps_k[:, 0, :], ACT.Square, accum_out=ssq[:, 1:2]).then_inc(k_sq, 1)
                    if has(s):
                        exps(s, j, g, 1)
                    if g == 0 and has(s - 1):
                        wait(act, rrep_mm, s)
                        wait(act, oT_lo_made, s - 1)
                        nc.scalar.copy(oT[:, :], ps_v[:, 0, :]).then_inc(rrep_made, 1)
                    if g == 1:
                        if has(s - 1):
                            wait(act, oT_made, s)
                            nc.scalar.copy(oT_hi[:, :, :], oT[:, :].rearrange("p (k t) -> p k t", k=KT)).then_inc(oT_hi_made, 1)
                    if g == v_group(s) and has(a):
                        wait(act, v_mm, a + 1)
                        wait(act, pv_mm, 4 * s)
                        if isinstance(s, int) and s < 3:
                            wait(act, cleared, 4)
                        nc.scalar.copy(v_ring[:, (j + 1) % RING, :], ps_v[:, 0, :]).then_inc(v_made, 1)

            steps(act, step)

        @block.vector
        def _(dve):
            def split_wqkv():
                for n in range(6):
                    c, i = divmod(n, 2)
                    part = (slice(None), slice(2 * i, 2 * i + 2), slice(c * H, (c + 1) * H))
                    dve.wait_ge(w_hi_made, n + 1)
                    nc.vector.tensor_tensor(wqkv_lo[part], wqkv_raw[part], wqkv_hi[part].bitcast(FP32), ALU.subtract).then_inc(w_lo_made, 1)
                dve.wait_ge(const_loaded, 16 * 4)

            def split_wo(k):
                dve.wait_ge(w_hi_made, 6 + k + 1)
                nc.vector.tensor_tensor(wo_lo[:, k, :], wo_raw[:, k, :], wo_hi[:, k, :].bitcast(FP32), ALU.subtract).then_inc(w_lo_made, 1)

            def tiled(ap):
                return ap.rearrange("p (k t) -> p k t", k=KT)

            def masked_scores(s, j, g, pair):
                m = early_masks[:, s, :] if isinstance(s, int) and s < 2 else mask[:, :]
                for h in (2 * pair, 2 * pair + 1):
                    head = 4 * g + h
                    wait_apart(dve, score_mm, NH * s + head + 1, passed["dve"])
                    nc.vector.tensor_tensor_reduce(
                        out=prob[:, g % 2, h, :], in0=score_ps[h % 2][:, 0, 0:WB * P], in1=m,
                        scale=-SCALE, scalar=3e38, op0=ALU.add, op1=ALU.min,
                        accum_out=nbias[:, j % 2, head:head + 1]).then_inc(masked, 1)

            def split_xT(b, slot):
                wait(dve, xT_hi_made, b + 1)
                nc.vector.tensor_tensor(xT_lo[:, slot, :, :], xT_in[:, :, :], xT_hi[:, slot, :, :].bitcast(FP32), ALU.subtract).then_inc(xT_lo_made, 1)

            split_xT(0, 0)
            split_wqkv()
            temp = probT[:, :, :, :].rearrange("p a b c -> p (a b c)")

            def step(s, j, turn):
                a = s + 1
                for g in range(GROUPS):
                    if g == 3 and has(s + 2):
                        split_xT(s + 2, j % 2)
                    if has(s) if g else has(s - 1):
                        G = 4 * s + g - 1
                        wait(dve, probT_mm, 2 * G + 1)
                        nc.vector.tensor_copy(probT[:, (g - 1) % 2, 0:2, :], probT_ps[:, :, 0:WB * P]).then_inc(probT_dve, 1)
                    if g == 0 and has(s - 1):
                        wait(dve, exp_made, NH * s)
                        nc.vector.reciprocal(rinv[:, :], rsum[:, (j - 1) % 2, :]).then_inc(rinv_made, 1)
                        wait(dve, rinv_made, s)
                        wait(dve, k_sq, s)
                        nc.vector.tensor_copy(scratch[:, :].rearrange("p (h d) -> p h d", d=HD), rinv[:, :].unsqueeze(2).to_broadcast([P, NH, HD])).then_inc(rinv_spread, 1)
                    if has(s):
                        masked_scores(s, j, g, 0)
                    if g == 2 and has(s - 1):
                        wait(dve, oT_hi_made, s)
                        nc.vector.tensor_tensor(oT_lo[:, :, :], tiled(oT[:, :]), oT_hi[:, :, :].bitcast(FP32), ALU.subtract).then_inc(oT_lo_made, 1)
                    if g == 2 and has(a):
                        wait(dve, k_rms, a + 1)
                        nc.vector.scalar_tensor_tensor(qk[:, 1, :], ps_k[:, 0, :], rms[:, 1:2], kw_b[:, :], ALU.mult, ALU.mult).then_inc(k_normed, 1)
                        if isinstance(a, int) and a == 0:
                            rotate(dve, nc.vector, 0, 0, 0, 1, temp[:, 0:H], temp[:, H:2 * H], k_normed, k_part, k_rot)
                    if isinstance(s, int) and s == 0:
                        split_wo(g)
                    if g == 0 and has(s - 2):
                        wait(dve, ln_rstd, s - 1)
                        if isinstance(s, int) and s > NB - 2:
                            wait(dve, x1_stored, 16 * (s - 3))
                        nc.vector.tensor_scalar(x1[:, j % 2, :], res[:, :], mv[:, 0:1], rstd[:, 0:1], ALU.subtract, ALU.mult).then_inc(x1_made, 1)
                    if g == 3 and has(s - 1):
                        wait(dve, wo_mm, s)
                        wait(dve, x1_made, s - 1)
                        wait(dve, x_loaded, 16 * s)
                        nc.vector.tensor_tensor(res[:, :], ps_v[:, 0, :], x_in[:, :], ALU.add).then_inc(res_made, 1)
                        wait(dve, res_made, s)
                        nc.vector.bn_stats(bn6[:, :], res[:, :]).then_inc(bn_made, 1)
                        wait_apart(dve, bn_made, s, passed["dve"])
                        nc.vector.bn_aggr(mv[:, :], bn6[:, :]).then_inc(mv_made, 1)
                    if g == 1 and has(a):
                        wait(dve, q_rms, a + 1)
                        nc.vector.scalar_tensor_tensor(qk[:, 0, :], ps_q[:, 0, :], rms[:, 0:1], qw_b[:, :], ALU.mult, ALU.mult).then_inc(q_normed, 1)
                        if isinstance(a, int) and a == 0:
                            rotate(dve, nc.vector, 0, 0, 0, 0, temp[:, 2 * H:3 * H], temp[:, 3 * H:4 * H], q_normed, q_part, q_rot)
                    if g == 3 and has(a):
                        wait(dve, qT_hi_made, a + 1)
                        nc.vector.tensor_tensor(qT_lo[:, (j + 1) % 2, :, :], tiled(ps_q[:, 0, :]), qT_hi[:, (j + 1) % 2, :, :].bitcast(FP32), ALU.subtract).then_inc(qT_lo_made, 1)
                    if g == 3 and has(a):
                        wait(dve, kT_hi_made, a + 1)
                        slot = key_slot(j + 1)
                        nc.vector.tensor_tensor(kT_lo[:, :, slot, :], tiled(ps_k[:, 0, :]), kT_hi[:, :, slot, :].bitcast(FP32), ALU.subtract).then_inc(kT_lo_made, 1)
                    if has(s):
                        masked_scores(s, j, g, 1)
                    if g == 1 and has(s - 1):
                        wait(dve, pv_mm, 4 * s)
                        wait(dve, rrep_made, s)
                        nc.vector.tensor_tensor(oT[:, :], oT_ps[:, 0, :], oT[:, :], ALU.mult).then_inc(oT_made, 1)

            steps(dve, step)

        @block.tensor
        def _(pe):
            def three(out, pairs):
                n = len(pairs)
                for i, (l, r) in enumerate(pairs):
                    last = nc.tensor.matmul(out, l, r, start=(i == 0), stop=(i == n - 1))
                return last

            def project(out, l_hi, l_lo, w_hi, w_lo, c, first=False):
                cols = slice(c * H, (c + 1) * H)
                if first:
                    for k in range(KT):
                        pe.wait_ge(w_lo_made, 2 * c + k // 2 + 1)
                        nc.tensor.matmul(out, l_hi[:, k, :], w_lo[:, k, cols], start=(k == 0), stop=False)
                        nc.tensor.matmul(out, l_hi[:, k, :], w_hi[:, k, cols], start=False, stop=False)
                        last = nc.tensor.matmul(out, l_lo[:, k, :], w_hi[:, k, cols], start=False, stop=(k == KT - 1))
                    return last
                return three(out, [p for k in range(KT) for p in (
                    (l_hi[:, k, :], w_lo[:, k, cols]), (l_hi[:, k, :], w_hi[:, k, cols]), (l_lo[:, k, :], w_hi[:, k, cols]))])

            def transposed(out, src):
                for k in range(KT):
                    last = nc.tensor.transpose(out[:, 0, k * P:(k + 1) * P], src[:, k * P:(k + 1) * P], ident[:, :])
                return last

            def scores(s, j, g, pair):
                for h in (2 * pair, 2 * pair + 1):
                    wait(pe, masked, NH * s + 4 * g + h - 1)
                    rows = slice(HD * h, HD * h + HD)
                    q_hi, q_lo = qT_hi[rows, j % 2, g, :], qT_lo[rows, j % 2, g, :]
                    seen = slice(window(j), window(j) + WB)
                    k_hi, k_lo = kT_hi[rows, g, seen, :], kT_lo[rows, g, seen, :]
                    three(score_ps[h % 2][:, 0, 0:WB * P], [(q_hi, k_lo), (q_hi, k_hi), (q_lo, k_hi)]).then_inc(score_mm, 1)

            def prob_transposes(G, g, pair):
                wait(pe, exp_made, 4 * G + 2 * pair + 2)
                if pair == 0:
                    wait(pe, probT_act, G)
                else:
                    wait(pe, probT_dve, G + 1)
                for h in range(2):
                    for w in range(WB):
                        last = nc.tensor.transpose(probT_ps[:, h, w * P:(w + 1) * P],
                                                   prob[:, g % 2, 2 * pair + h, w * P:(w + 1) * P], ident[:, :])
                last.then_inc(probT_mm, 1)

            def values(s, j, g):
                G = 4 * s + g
                if g == 0:
                    wait(pe, v_made, s + 1)
                    wait(pe, oT_made, s)
                wait(pe, probT_act, G + 1)
                for w in range(WB):
                    slot = (window(j) + w) % RING
                    for h in range(4):
                        head = 4 * g + h
                        last = nc.tensor.matmul(oT_ps[HD * h:HD * h + HD, 0, g * P:(g + 1) * P],
                                                v_ring[:, slot, head * HD:(head + 1) * HD],
                                                probT[:, g % 2, h, w * P:(w + 1) * P],
                                                start=(w == 0), stop=(w == WB - 1))
                last.then_inc(pv_mm, 1)

            pe.wait_ge(ident_loaded, 16)

            def step(s, j, turn):
                a = s + 1
                for g in range(GROUPS):
                    behind = has(s) if g else has(s - 1)
                    is_first = isinstance(s, int) and s == -1
                    x_hi, x_lo = xT_hi[:, (j + 1) % 2, :, :], xT_lo[:, (j + 1) % 2, :, :]
                    if behind:
                        prob_transposes(4 * s + g - 1, (g - 1) % 4, 0)
                    if has(s):
                        if g == 0:
                            wait(pe, kT_lo_made, s + 1)
                            if window(j) == 0:
                                wait(pe, kT_copied, 4 * (turn + 1))
                            if isinstance(s, int) and s == 0:
                                wait(pe, cleared, 4)
                        scores(s, j, g, 0)
                    if g == 0 and has(a):
                        wait(pe, xT_lo_made, a + 1)
                        wait(pe, qT_lo_made, a)
                        project(ps_q[:, 0, :], x_hi, x_lo, wqkv_hi, wqkv_lo, 0, is_first).then_inc(q_mm, 1)
                    if g == 3 and has(a):
                        wait(pe, q_rot, a + 1)
                        transposed(ps_q, qk[:, 0, :]).then_inc(qT_mm, 1)
                    if behind:
                        prob_transposes(4 * s + g - 1, (g - 1) % 4, 1)
                    if g == 0 and has(s - 1):
                        wait(pe, rinv_spread, s)
                        wait(pe, res_made, s - 1)
                        wait(pe, v_made, s + 1 if has(s) else NB)
                        for k in range(KT):
                            last = nc.tensor.transpose(ps_v[:, 0, k * P:(k + 1) * P], scratch[:, k * P:(k + 1) * P], ident[:, :])
                        last.then_inc(rrep_mm, 1)
                    if g == 1 and has(a):
                        wait(pe, x1T_made, s - 1)
                        project(ps_k[:, 0, :], x_hi, x_lo, wqkv_hi, wqkv_lo, 1, is_first).then_inc(k_mm, 1)
                    if g == 3 and has(a):
                        wait(pe, k_rot, a + 1)
                        transposed(ps_k, qk[:, 1, :]).then_inc(kT_mm, 1)
                    if has(s):
                        scores(s, j, g, 1)
                    if g < 2 and has(s - 1):
                        values(s - 1, (j - 1) % RING, g + 2)
                    if g >= 2 and has(s):
                        values(s, j, g - 2)
                    if g == 0 and has(s - 2):
                        wait(pe, x1_made, s - 1)
                        wait(pe, kT_lo_made, s + 1 if has(s) else NB)
                        transposed(ps_k, x1[:, j % 2, :]).then_inc(x1T_mm, 1)
                    if g == v_group(s) and has(a):
                        wait(pe, res_made, s)
                        project(ps_v[:, 0, :], x_hi, x_lo, wqkv_hi, wqkv_lo, 2, is_first).then_inc(v_mm, 1)
                    if g == 2 and has(s - 1):
                        wait(pe, oT_lo_made, s)
                        wait(pe, rrep_made, s)
                        if isinstance(s, int) and s == 1:
                            wait(pe, w_lo_made, 6 + KT)
                        project(ps_v[:, 0, :], oT_hi, oT_lo, wo_hi, wo_lo, 0).then_inc(wo_mm, 1)

            steps(pe, step)


def constants():
    inv_freq = (np.float32(1.0) / np.float32(THETA) ** (np.arange(0, HD, 2, dtype=np.float32) / np.float32(HD))).astype(np.float32)
    freqs = np.arange(S, dtype=np.float32)[:, None] * inv_freq[None, :]
    cos, sin = np.cos(freqs), np.sin(freqs)
    trig = np.stack([np.concatenate([cos, cos], 1), np.concatenate([-sin, sin], 1)], 1).astype(np.float32)
    q, k = np.arange(P)[:, None], np.arange(WB * P)[None, :]
    d = q + (WB - 1) * P - k
    seen = (d >= 0) & (d < WINDOW)
    masks = np.stack([np.where(seen & (k >= first * P), 0.0, NEG) for first in (2, 1, 0)], 1).astype(np.float32)
    return trig, np.eye(P, dtype=np.float32), masks


def ffn_phase(nc, W_router_gate, Ws_gu, Ws_down, We_gu, We_down, ident_in, index_in, x1_dram, factor_dram, x1T, gu_raw, gu_loaded, out):
    TN = 512
    NT = S // TN
    BT = TN // P
    UN = (I_SH + E * I_MOE) // P
    NCH = UN // UNITS
    PER = UNITS * NT
    HRING = 4
    LOW = 16
    RR = 4
    GR = 32

    with ExitStack() as ctx:
        def sb(name, shape, dt=FP32):
            return ctx.enter_context(nc.sbuf_tensor(name, shape, dt))

        def sem(name):
            return ctx.enter_context(nc.semaphore(name))

        x_hi, x_lo = sb("x_hi", [P, KT, S], FP32R), sb("x_lo", [P, KT, S], FP32R)
        wd_raw = sb("wd_raw", [P, UNITS, H])
        gu_hi, gu_lo = sb("gu_hi", [P, 2, KT, 2 * CW], FP32R), sb("gu_lo", [P, 2, KT, 2 * CW], FP32R)
        wd_hi, wd_lo = sb("wd_hi", [P, UNITS, H], FP32R), sb("wd_lo", [P, UNITS, H], FP32R)
        h_hi, h_lo = sb("h_hi", [P, HRING, TN], FP32R), sb("h_lo", [P, HRING, TN], FP32R)
        work = sb("work", [P, 4, TN])
        factor = sb("factor", [P, RR, TN])
        first_raw = factor[:, :, :].rearrange("p r n -> p (r n)")[:, 0:KT // 2 * 2 * CW].rearrange("p (k n) -> p k n", n=2 * CW)
        r_raw = sb("r_raw", [P, KT, NR])
        r_hi, r_both = (t[:, HRING - 1, :].rearrange("p (k m) -> p k m", k=KT) for t in (h_hi, h_lo))
        ident2 = sb("ident2", [P, P])
        index8 = sb("index8", [P, E])
        logits = sb("logits", [P, NB, NR])
        top = sb("top", [P, NB, 8])
        top_at = sb("top_at", [P, NB, 8], mybir.dt.uint32)
        top_f = sb("top_f", [P, NB, TOP_K])
        hit = sb("hit", [P, TOP_K, NB, E])
        red = sb("red", [P, 2, NB])
        combine = sb("combine", [P, NB, NR])
        bn6, mv, rstd = sb("bn6_y", [P, 2, 6]), sb("mv_y", [P, 2, 2]), sb("rstd_y", [P, 2, 2])
        half = sb("half_y", [P, 1])
        y = x1T[:, :, :].rearrange("p k s -> p (k s)").rearrange("p (b n) -> p b n", n=H)

        def bank(name):
            return ctx.enter_context(nc.psum_tensor(name, [P, TN], FP32))

        gate_ps = [bank(f"gate_ps{i}") for i in range(2)]
        up_ps = [bank(f"up_ps{i}") for i in range(2)]
        down_ps = [bank(f"down_ps{i}") for i in range(BT)]

        wd_loaded, y_loaded, small_loaded, stored = map(sem, ("wd_loaded", "y_loaded", "small_loaded", "stored"))
        x_hi_made, x_lo_made, r_hi_made, r_lo_made, r_cleared = map(sem, ("x_hi_made", "x_lo_made", "r_hi_made", "r_lo_made", "r_cleared"))
        gu_hi_made, gu_lo_made, wd_hi_made, wd_lo_made = map(sem, ("gu_hi_made", "gu_lo_made", "wd_hi_made", "wd_lo_made"))
        gate_mm, up_mm, down_mm, logitT_mm, logit_mm = map(sem, ("gate_mm", "up_mm", "down_mm", "logitT_mm", "logit_mm"))
        silu_made, up_scaled, h_made, h_hi_made, h_lo_made, y_added = map(sem, ("silu_made", "up_scaled", "h_made", "h_hi_made", "h_lo_made", "y_added"))
        logitT_made, exp_made, route, combine_made = map(sem, ("logitT_made", "router_exp_made", "route", "combine_made"))
        shared_made = sem("shared_made")
        combineT_mm, combineT_made, factors_stored = map(sem, ("combineT_mm", "combineT_made", "factors_stored"))
        factor_loaded = [sem(f"factor_loaded{i}") for i in range(RR)]
        y_bn, y_mv, y_var, y_rstd, y_normed, pool_ready = map(sem, ("y_bn", "y_mv", "y_var", "y_rstd", "y_normed", "pool_ready"))

        def chunks(engine, chunk):
            for c in (0, 1):
                chunk(c, c)
            with engine.Fori(0, (NCH - 3) // 2) as i:
                for k in (2, 3):
                    chunk(2 * i + k, k % 2)
            chunk(NCH - 1, (NCH - 1) % 2)

        def is_chunk(c, n):
            return isinstance(c, int) and c == n

        def raw_gu(c, k):
            return first_raw[:, k - KT // 2, :] if is_chunk(c, 0) and k >= KT // 2 else gu_raw[:, k % 2, :]

        X_PARTS = [(slice(k, k + 1), slice(0, TN)) for k in range(KT)] + [(slice(0, KT), slice(tt * TN, (tt + 1) * TN)) for tt in range(1, NT)]

        block = ctx.enter_context(nc.Block())

        @block.sync
        def _(sp):
            def parts(c):
                return pieces(c, Ws_gu, Ws_down, We_gu, We_down)

            def load_wd(c):
                cuts = {0, P, 2 * P, CW} | {at for at, *_ in parts(c)}
                if len(cuts) == 4:
                    cuts.add(P // 2)
                cuts = sorted(cuts)
                for lo, hi in zip(cuts, cuts[1:]):
                    at, _, _, _, dn, col = [p for p in parts(c) if p[0] <= lo][-1]
                    sp.dma_start(wd_raw[lo % P:lo % P + hi - lo, lo // P, :], dn[col + lo - at:col + hi - at, :]).then_inc(wd_loaded, 16)

            load_gu(sp, first_raw, parts(0), 1, gu_loaded)
            sp.dma_start(r_raw[:, :, :], W_router_gate.rearrange("(k p) n -> p k n", p=P)).then_inc(small_loaded, 16)
            sp.dma_start(ident2[:, :], ident_in).then_inc(small_loaded, 16)
            sp.dma_start(index8[:, :], index_in).then_inc(small_loaded, 16)
            load_wd(0)
            sp.wait_ge(x_lo_made, len(X_PARTS))
            sp.dma_start(y, x1_dram.rearrange("(b p) n -> p b n", p=P)).then_inc(y_loaded, 16)

            for c in range(1, NCH):
                sp.wait_ge(gu_lo_made, KT * c)
                load_gu(sp, gu_raw, parts(c), 0, gu_loaded)
                sp.wait_ge(wd_lo_made, UNITS * c)
                load_wd(c)
                sp.wait_ge(gu_lo_made, KT * c + KT // 2)
                load_gu(sp, gu_raw, parts(c), 1, gu_loaded)
                if c == 1:
                    for tt in range(NT):
                        sp.wait_ge(combineT_made, tt + 1)
                        cols = slice(tt * TN, (tt + 1) * TN)
                        shared = factor[E:E + 1, tt, :].unsqueeze(1).to_broadcast([1, I_SH // GR, TN])
                        routed = factor[0:E, tt, :].unsqueeze(1).to_broadcast([E, I_MOE // GR, TN])
                        sp.dma_start(factor_dram[0:I_SH // GR, cols].unsqueeze(0), shared).then_inc(factors_stored, 16)
                        sp.dma_start(factor_dram[I_SH // GR:, cols].rearrange("(e j) n -> e j n", e=E), routed).then_inc(factors_stored, 16)

            out_v = out.rearrange("(b p) n -> b p n", p=P)
            for b in range(NB):
                wait(sp, y_normed, b + 1)
                sp.dma_start(out_v[b], y[:, b, :]).then_inc(stored, 16)
            sp.wait_ge(stored, 16 * NB)

        @block.gpsimd
        def _(pool):
            pool.memset(r_hi[:, :, :].bitcast(FP32), 0.0).then_inc(r_cleared, 1)
            pool.memset(r_both[:, :, :].bitcast(FP32), 0.0).then_inc(r_cleared, 1)
            pool.memset(half[:, :], -0.5).then_inc(pool_ready, 1)
            pool.wait_ge(pool_ready, 1)
            for b in range(NB):
                pool.wait_ge(y_mv, b + 1)
                nc.gpsimd.tensor_scalar(rstd[:, b % 2, 1:2], mv[:, b % 2, 1:2], 1.0, LN_EPS, ALU.mult, ALU.add).then_inc(y_var, 1)
                pool.wait_ge(y_var, b + 1)
                nc.gpsimd.tensor_tensor(rstd[:, b % 2, 0:1], rstd[:, b % 2, 1:2], half[:, :], ALU.pow).then_inc(y_rstd, 1)

        @block.scalar
        def _(act):
            def split_x(i):
                ks, cols = X_PARTS[i]
                nc.scalar.copy(x_hi[:, ks, cols], x1T[:, ks, cols]).then_inc(x_hi_made, 1)

            def split_router():
                act.wait_ge(small_loaded, 48)
                act.wait_ge(r_cleared, 2)
                nc.scalar.copy(r_hi[:, :, 0:NR], r_raw[:, :, :]).then_inc(r_hi_made, 1)

            def split_gu(c, par, ks):
                for k in ks:
                    wait(act, gu_loaded, 16 * GU_LOADS * (2 * c + k // 2 + 1))
                    nc.scalar.copy(gu_hi[:, par, k, :], raw_gu(c, k)).then_inc(gu_hi_made, 1)

            def split_wd(c):
                wait(act, wd_loaded, 64 * (c + 1))
                wait(act, down_mm, BT * NT * c)
                for u in range(UNITS):
                    nc.scalar.copy(wd_hi[:, u, :], wd_raw[:, u, :]).then_inc(wd_hi_made, 1)

            def load_factor(c, m):
                cc, m = (c, m) if m < PER else (c + 1, m - PER)
                if isinstance(cc, int) and not 0 < cc < NCH:
                    return
                tt, u = divmod(m, UNITS)
                if is_chunk(cc, 1) and m == 0:
                    act.wait_ge(factors_stored, 32 * NT)
                if not (is_chunk(cc, 1) and m < RR):
                    wait(act, up_scaled, PER * (cc - 1) + m - RR + 1)
                first_row = P // GR * (UNITS * cc + u)
                src = factor_dram[bass.ds(first_row, P // GR), tt * TN:(tt + 1) * TN]
                act.dma_start(factor[:, m % RR, :], src.unsqueeze(1).to_broadcast([P // GR, GR, TN])).then_inc(factor_loaded[m % RR], 16)

            def router(tt):
                if tt == 0:
                    act.wait_ge(gu_lo_made, KT)
                    for i in range(NT):
                        act.wait_ge(logitT_mm, i + 1)
                        nc.scalar.copy(factor[0:LOW + NR, i, :], down_ps[i][0:LOW + NR, :]).then_inc(logitT_made, 1)
                if tt == 2:
                    for i in range(NT):
                        act.wait_ge(combineT_mm, i + 1)
                        nc.scalar.copy(factor[0:NR, i, :], down_ps[i][0:NR, :]).then_inc(combineT_made, 1)

            for k in range(KT):
                split_gu(0, 0, [k])
                split_x(k)
            split_x(KT)

            def chunk(c, par):
                for tt in range(NT):
                    for u in range(UNITS):
                        m = UNITS * tt + u
                        n = PER * c + m
                        wait(act, gate_mm, n + 1)
                        wait(act, h_made, n - 1)
                        nc.scalar.activation(work[:, m % 2, :], gate_ps[m % 2][:, :], ACT.Silu).then_inc(silu_made, 1)
                        load_factor(c, m + RR - 1)
                        wait(act, h_made, n + 1)
                        wait(act, down_mm, BT * (NT * c + tt + (u - HRING) // UNITS + 1))
                        nc.scalar.copy(h_hi[:, m % HRING, :], work[:, 2 + m % 2, :]).then_inc(h_hi_made, 1)
                        if is_chunk(c, 0) and tt == 0 and u != 1:
                            split_x(KT + 1 + u // 2)
                        if is_chunk(c, 0) and tt == 0 and u == 0:
                            split_router()
                        if tt == 0 and u == 1:
                            split_wd(c)
                        if tt >= 1 and u == 1 and not is_chunk(c, NCH - 1):
                            split_gu(c + 1, 1 - par, {1: (0, 1), 2: (2,), 3: (3,)}[tt])
                        if is_chunk(c, 0) and tt == 1 and u == 0:
                            act.wait_ge(route, 4)
                            nc.scalar.activation(logits[:, :, :], logits[:, :, :], ACT.Exp).then_inc(exp_made, 1)
                    if is_chunk(c, 0):
                        router(tt)

            chunks(act, chunk)

        @block.vector
        def _(dve):
            def split_x(i):
                ks, cols = X_PARTS[i]
                dve.wait_ge(x_hi_made, i + 1)
                nc.vector.tensor_tensor(x_lo[:, ks, cols], x1T[:, ks, cols], x_hi[:, ks, cols].bitcast(FP32), ALU.subtract).then_inc(x_lo_made, 1)

            def split_router():
                dve.wait_ge(r_hi_made, 1)
                nc.vector.tensor_copy(r_both[:, :, 0:NR], r_hi[:, :, 0:NR])
                nc.vector.tensor_tensor(r_both[:, :, LOW:LOW + NR], r_raw[:, :, :], r_hi[:, :, 0:NR].bitcast(FP32), ALU.subtract).then_inc(r_lo_made, 1)

            def split_gu(c, par, ks):
                for k in ks:
                    wait(dve, gu_hi_made, KT * c + k + 1)
                    nc.vector.tensor_tensor(gu_lo[:, par, k, :], raw_gu(c, k), gu_hi[:, par, k, :].bitcast(FP32), ALU.subtract).then_inc(gu_lo_made, 1)

            def split_wd(c):
                for u in range(UNITS):
                    wait(dve, wd_hi_made, UNITS * c + u + 1)
                    nc.vector.tensor_tensor(wd_lo[:, u, :], wd_raw[:, u, :], wd_hi[:, u, :].bitcast(FP32), ALU.subtract).then_inc(wd_lo_made, 1)

            steps_done = [0]

            def link(instruction):
                steps_done[0] += 1
                instruction.then_inc(route, 1)
                dve.wait_ge(route, steps_done[0])

            def router_logits():
                dve.wait_ge(logit_mm, 1)
                parts = down_ps[0][:, :].rearrange("p (b n) -> p b n", n=2 * LOW)
                link(nc.vector.tensor_copy(logits[:, :, :], parts[:, :, LOW:LOW + NR]))
                link(nc.vector.tensor_tensor(logits[:, :, :], parts[:, :, 0:NR], logits[:, :, :], ALU.add))
                link(nc.vector.tensor_reduce(red[:, 0, :], logits[:, :, 0:E], mybir.AxisListType.X, ALU.max))
                nc.vector.tensor_scalar(logits[:, :, E], logits[:, :, E], -1.0, None, ALU.mult)
                link(nc.vector.tensor_tensor(logits[:, :, 0:E], logits[:, :, 0:E], red[:, 0, :].unsqueeze(2).to_broadcast([P, NB, E]), ALU.subtract))

            def router_probs():
                dve.wait_ge(exp_made, 1)
                link(nc.vector.tensor_reduce(red[:, 0, :], logits[:, :, 0:E], mybir.AxisListType.X, ALU.add))
                link(nc.vector.reciprocal(red[:, 1, :], red[:, 0, :]))
                link(nc.vector.tensor_tensor(logits[:, :, 0:E], logits[:, :, 0:E], red[:, 1, :].unsqueeze(2).to_broadcast([P, NB, E]), ALU.mult))
                link(nc.vector.tensor_scalar(red[:, 0, :], logits[:, :, E], 1.0, None, ALU.add))
                nc.vector.reciprocal(combine[:, :, E], red[:, 0, :]).then_inc(shared_made, 1)
                for b in range(NB):
                    last = nc.vector.max(top[:, b, :], logits[:, b, 0:E])
                link(last)

            def router_top():
                for b in range(NB):
                    last = nc.vector.max_index(top_at[:, b, :], top[:, b, :], logits[:, b, 0:E])
                link(last)
                link(nc.vector.tensor_copy(top_f[:, :, :], top_at[:, :, 0:TOP_K]))
                for t in range(TOP_K):
                    last = nc.vector.tensor_tensor(hit[:, t, :, :], top_f[:, :, t:t + 1].to_broadcast([P, NB, E]),
                                                   index8[:, :].unsqueeze(1).to_broadcast([P, NB, E]), ALU.is_equal)
                link(last)
                link(nc.vector.tensor_tensor(hit[:, 0, :, :], hit[:, 0, :, :], hit[:, 1, :, :], ALU.add))
                nc.vector.tensor_tensor(combine[:, :, 0:E], logits[:, :, 0:E], hit[:, 0, :, :], ALU.mult).then_inc(combine_made, 1)

            for k in range(KT):
                split_gu(0, 0, [k])
                split_x(k)
            split_x(KT)

            def add_down(c, tt):
                turn = NT * c + tt
                for i in range(BT):
                    b = BT * tt + i
                    wait(dve, down_mm, BT * turn + i + 1)
                    if i == 0:
                        wait(dve, y_added, BT * (turn - NT + 1))
                        if is_chunk(c, 0) and tt == 0:
                            dve.wait_ge(y_loaded, 16)
                            dve.wait_ge(shared_made, 1)
                    if is_chunk(c, 0):
                        nc.vector.scalar_tensor_tensor(y[:, b, :], down_ps[i][:, :], combine[:, b, E:E + 1], y[:, b, :], ALU.mult, ALU.add).then_inc(y_added, 1)
                    else:
                        nc.vector.tensor_tensor(y[:, b, :], down_ps[i][:, :], y[:, b, :], ALU.add).then_inc(y_added, 1)

            def normalise(b):
                dve.wait_ge(y_added, BT * NT * (NCH - 1) + b + 1)
                nc.vector.bn_stats(bn6[:, b % 2, :], y[:, b, :]).then_inc(y_bn, 1)
                dve.wait_ge(y_bn, b + 1)
                nc.vector.bn_aggr(mv[:, b % 2, :], bn6[:, b % 2, :]).then_inc(y_mv, 1)

            def finish(b):
                dve.wait_ge(y_mv, b + 1)
                dve.wait_ge(y_rstd, b + 1)
                nc.vector.tensor_scalar(y[:, b, :], y[:, b, :], mv[:, b % 2, 0:1], rstd[:, b % 2, 0:1], ALU.subtract, ALU.mult).then_inc(y_normed, 1)

            def chunk(c, par):
                for tt in range(NT):
                    for u in range(UNITS):
                        m = UNITS * tt + u
                        n = PER * c + m
                        h = work[:, 2 + m % 2, :]
                        wait(dve, up_mm, n + 1)
                        wait(dve, h_lo_made, n - 1)
                        if is_chunk(c, 0):
                            wait(dve, silu_made, n + 1)
                            nc.vector.tensor_tensor(h, work[:, m % 2, :], up_ps[m % 2][:, :], ALU.mult).then_inc(h_made, 1)
                        else:
                            wait(dve, factor_loaded[m % RR], 16 * (PER // RR * (c - 1) + m // RR + 1))
                            nc.vector.tensor_tensor(h, up_ps[m % 2][:, :], factor[:, m % RR, :], ALU.mult).then_inc(up_scaled, 1)
                            wait(dve, silu_made, n + 1)
                            wait(dve, up_scaled, n - PER + 1)
                            nc.vector.tensor_tensor(h, work[:, m % 2, :], h, ALU.mult).then_inc(h_made, 1)
                        wait(dve, h_hi_made, n + 1)
                        nc.vector.tensor_tensor(h_lo[:, m % HRING, :], h, h_hi[:, m % HRING, :].bitcast(FP32), ALU.subtract).then_inc(h_lo_made, 1)
                        if is_chunk(c, 0) and tt == 0 and u != 1:
                            split_x(KT + 1 + u // 2)
                        if is_chunk(c, 0) and tt == 0 and u == 0:
                            split_router()
                        if is_chunk(c, 0) and tt == 1:
                            (router_logits, router_probs, lambda: add_down(0, 0))[u]()
                        elif u == 0 and tt:
                            add_down(c, tt - 1)
                            if is_chunk(c, 0) and tt == 2:
                                router_top()
                            if is_chunk(c, NCH - 1):
                                for b in range(BT * (tt - 1), BT * tt):
                                    normalise(b)
                                    if b % 2:
                                        finish(b - 1)
                                        finish(b)
                        elif u == 0 and not is_chunk(c, 0):
                            add_down(c - 1, NT - 1)
                        if u == 1 and tt == 0:
                            split_wd(c)
                        if tt >= 1 and u == 1 and not is_chunk(c, NCH - 1):
                            split_gu(c + 1, 1 - par, {1: (0, 1), 2: (2,), 3: (3,)}[tt])

            chunks(dve, chunk)
            for i in range(BT):
                b = BT * (NT - 1) + i
                turn = NT * NCH - 1
                dve.wait_ge(down_mm, BT * turn + i + 1)
                nc.vector.tensor_tensor(y[:, b, :], down_ps[i][:, :], y[:, b, :], ALU.add).then_inc(y_added, 1)
                normalise(b)
                if i:
                    finish(b - 1)
            finish(NB - 1)

        @block.tensor
        def _(pe):
            def router():
                pe.wait_ge(r_lo_made, 1)
                for tt in range(NT):
                    pe.wait_ge(x_lo_made, KT + tt)
                    cols = slice(tt * TN, (tt + 1) * TN)
                    for k in range(KT):
                        nc.tensor.matmul(down_ps[tt][:, :], r_hi[:, k, :], x_lo[:, k, cols], start=(k == 0), stop=False)
                        last = nc.tensor.matmul(down_ps[tt][:, :], r_both[:, k, :], x_hi[:, k, cols], start=False, stop=(k == KT - 1))
                    last.then_inc(logitT_mm, 1)

            def router_rows():
                pe.wait_ge(small_loaded, 48)
                for b in range(NB):
                    pe.wait_ge(logitT_made, b // BT + 1)
                    last = nc.tensor.transpose(down_ps[0][:, 2 * LOW * b:2 * LOW * b + LOW + NR], factor[0:LOW + NR, b // BT, (b % BT) * P:(b % BT + 1) * P], ident2[0:LOW + NR, 0:LOW + NR])
                last.then_inc(logit_mm, 1)

            def gate_up(c, par, tt, u):
                m = UNITS * tt + u
                cols = slice(tt * TN, (tt + 1) * TN)
                wait(pe, h_made, PER * c + m - 1)
                for ps, base, done in ((gate_ps, 0, gate_mm), (up_ps, CW, up_mm)):
                    o = ps[m % 2][:, :]
                    part = slice(base + u * P, base + (u + 1) * P)
                    for k in range(KT):
                        if m == 0 and base == 0:
                            wait(pe, gu_lo_made, KT * c + k + 1)
                        if is_chunk(c, 0) and u == 0 and base == 0:
                            pe.wait_ge(x_lo_made, KT + tt if tt else k + 1)
                        nc.tensor.matmul(o, gu_lo[:, par, k, part], x_hi[:, k, cols], start=(k == 0), stop=False)
                        nc.tensor.matmul(o, gu_hi[:, par, k, part], x_lo[:, k, cols], start=False, stop=False)
                        last = nc.tensor.matmul(o, gu_hi[:, par, k, part], x_hi[:, k, cols], start=False, stop=(k == KT - 1))
                    last.then_inc(done, 1)

            def down(c, tt):
                turn = NT * c + tt
                wait(pe, h_lo_made, UNITS * (turn + 1))
                if tt == 0:
                    wait(pe, wd_lo_made, UNITS * (c + 1))
                if is_chunk(c, 0) and tt == 0:
                    pe.wait_ge(route, 2)
                if is_chunk(c, 0) and tt == 2:
                    pe.wait_ge(combineT_made, NT)
                for i in range(BT):
                    wait(pe, y_added, BT * (turn - 1) + i + 1)
                    tok = slice(i * P, (i + 1) * P)
                    for u in range(UNITS):
                        slot = (UNITS * tt + u) % HRING
                        hh, hl = h_hi[:, slot, tok], h_lo[:, slot, tok]
                        nc.tensor.matmul(down_ps[i][:, :], hl, wd_hi[:, u, :], start=(u == 0), stop=False)
                        nc.tensor.matmul(down_ps[i][:, :], hh, wd_lo[:, u, :], start=False, stop=False)
                        last = nc.tensor.matmul(down_ps[i][:, :], hh, wd_hi[:, u, :], start=False, stop=(u == UNITS - 1))
                    last.then_inc(down_mm, 1)

            def chunk(c, par):
                for tt in range(NT):
                    for u in range(UNITS):
                        gate_up(c, par, tt, u)
                        if is_chunk(c, 0) and tt == 1 and u == 0:
                            router_rows()
                        if u == 0 and tt:
                            down(c, tt - 1)
                        elif u == 0 and not is_chunk(c, 0):
                            down(c - 1, NT - 1)
                    if tt == 0 and is_chunk(c, 0):
                        router()
                    if tt == 2 and is_chunk(c, 0):
                        pe.wait_ge(combine_made, 1)
                        for i in range(NT):
                            pe.wait_ge(y_added, BT + i + 1)
                            for b in range(BT * i, BT * (i + 1)):
                                last = nc.tensor.transpose(down_ps[i][0:NR, (b % BT) * P:(b % BT + 1) * P], combine[:, b, :], ident2[:, :])
                            last.then_inc(combineT_mm, 1)

            def last_down():
                turn = NT * NCH - 1
                for units in (range(UNITS - 1), range(UNITS - 1, UNITS)):
                    pe.wait_ge(h_lo_made, UNITS * turn + units[-1] + 1)
                    for i in range(BT):
                        if units[0] == 0:
                            pe.wait_ge(y_added, BT * (turn - 1) + i + 1)
                        tok = slice(i * P, (i + 1) * P)
                        for u in units:
                            slot = (UNITS * (NT - 1) + u) % HRING
                            hh, hl = h_hi[:, slot, tok], h_lo[:, slot, tok]
                            nc.tensor.matmul(down_ps[i][:, :], hl, wd_hi[:, u, :], start=(u == 0), stop=False)
                            nc.tensor.matmul(down_ps[i][:, :], hh, wd_lo[:, u, :], start=False, stop=False)
                            last = nc.tensor.matmul(down_ps[i][:, :], hh, wd_hi[:, u, :], start=False, stop=(u == UNITS - 1))
                        if units[-1] == UNITS - 1:
                            last.then_inc(down_mm, 1)

            chunks(pe, chunk)
            last_down()




def kernel(L0_attn_hidden_states, L0_attn_Wqkv, L0_attn_q_norm_w, L0_attn_k_norm_w, L0_attn_Wo,
           L0_ffn_W_router, L0_ffn_W_sgate, L0_ffn_Ws_gate_up, L0_ffn_Ws_down, L0_ffn_We_gate_up, L0_ffn_We_down):
    import concourse.bacc as bacc
    from concourse.bass_utils import run_bass_kernel_spmd

    trig, ident, masks = constants()
    nc = bacc.Bacc("TRN2", target_bir_lowering=False, num_devices=1)
    arrays = {
        "x": np.asarray(L0_attn_hidden_states).reshape(S, H),
        "xT": np.asarray(L0_attn_hidden_states).reshape(S, H).T,
        "Wqkv": L0_attn_Wqkv, "q_w": L0_attn_q_norm_w, "k_w": L0_attn_k_norm_w, "Wo": L0_attn_Wo,
        "W_router_gate": np.concatenate([np.asarray(L0_ffn_W_router), np.asarray(L0_ffn_W_sgate)], 0).T,
        "Ws_gu": L0_ffn_Ws_gate_up, "Ws_down": L0_ffn_Ws_down, "We_gu": L0_ffn_We_gate_up, "We_down": L0_ffn_We_down,
        "trig": trig, "ident_c": ident, "masks_c": masks,
        "index_c": np.tile(np.arange(E, dtype=np.float32), (P, 1)),
    }
    arrays = {f"in_{n}": np.ascontiguousarray(a) for n, a in arrays.items()}
    a = {n[3:]: nc.dram_tensor(n, v.shape, mybir.dt.from_np(v.dtype), kind="ExternalInput").ap() for n, v in arrays.items()}
    out = nc.dram_tensor("out_dram", (S, H), FP32, kind="ExternalOutput").ap()
    x1_dram = nc.dram_tensor("x1_dram", (S, H), FP32, kind="Internal").ap()
    factor_dram = nc.dram_tensor("factor_dram", ((I_SH + E * I_MOE) // 32, S), FP32, kind="Internal").ap()
    with nc.sbuf_tensor("x1T", [P, KT, S], FP32) as x1T, nc.sbuf_tensor("gu_raw", [P, KT // 2, 2 * CW], FP32) as gu_raw, \
            nc.semaphore("gu_loaded") as gu_loaded:

        def load_ahead(sp):
            load_gu(sp, gu_raw, pieces(0, a["Ws_gu"], a["Ws_down"], a["We_gu"], a["We_down"]), 0, gu_loaded)

        attention_phase(nc, a["x"], a["xT"], a["Wqkv"], a["q_w"], a["k_w"], a["Wo"], a["trig"], a["ident_c"], a["masks_c"], x1_dram, x1T, load_ahead)
        ffn_phase(nc, a["W_router_gate"], a["Ws_gu"], a["Ws_down"], a["We_gu"], a["We_down"], a["ident_c"], a["index_c"],
                  x1_dram, factor_dram, x1T, gu_raw, gu_loaded, out)
    r = run_bass_kernel_spmd(nc, [arrays], core_ids=[0])
    return r.results[0]["out_dram"].reshape(1, S, H)
```
